# Optimizing a Trainium2 kernel written in Bass

```python
import numpy as np
import jax
import jax.numpy as jnp

def _softmax(x, axis=-1):
    return jax.nn.softmax(x, axis=axis)

def _gelu(x):
    return jax.nn.gelu(x, approximate=True)

def _silu(x):
    return jax.nn.silu(x)

def _sigmoid(x):
    return jax.nn.sigmoid(x)

def _layernorm(x, axis=-1, eps=1e-05):
    m = jnp.mean(x, axis=axis, keepdims=True)
    v = jnp.var(x, axis=axis, keepdims=True)
    return (x - m) / jnp.sqrt(v + eps)

def _scatter_add(tgt, idx, src, axis=0):
    return tgt.at[idx].add(src)

def _segment_sum(src, seg, n):
    return jax.ops.segment_sum(src, seg, n)
kernel_name = 'mk_xattn_ffn_d1_seqx_r8_f5f931'

def setup_inputs(seed: int=0):
    np.random.seed(seed)
    _w = jnp.asarray

    def _rec_inputs():
        import jax
        import jax.numpy as jnp
        _rk = jax.random.key(seed)
        x = -0.0002928 + 1 * jax.random.normal(jax.random.fold_in(_rk, 1), (4, 512, 128), jnp.float32)
        _lenS = 512 - jax.random.randint(jax.random.fold_in(_rk, 7), (4,), 0, max(1, 512 // 4) + 1, jnp.int32)
        _lenS2 = 77 - jax.random.randint(jax.random.fold_in(_rk, 8), (4,), 0, max(1, 77 // 4) + 1, jnp.int32)
        _ctx_1024P = jax.random.normal(jax.random.fold_in(_rk, 11), (4, 16, 128), jnp.float32)
        _ctx_1024c = jax.random.dirichlet(jax.random.fold_in(_rk, 511), 0.3 * jnp.ones((16,), jnp.float32), (4, 77))
        _ctx_1024t = jnp.einsum('bsk,bkd->bsd', _ctx_1024c, _ctx_1024P)
        _ctx_1024t = _ctx_1024t * jax.lax.rsqrt(jnp.mean(jnp.square(_ctx_1024t)) + 1e-12) * 0.953939
        ctx_1024 = -1.39393e-06 + 0.999914 * (_ctx_1024t + 0.3 * jax.random.normal(jax.random.fold_in(_rk, 611), (4, 77, 128), jnp.float32))
        return (x, ctx_1024)
    x, ctx_1024 = _rec_inputs()

    def _L0_xattn_setup():
        import jax, jax.numpy as jnp
        import numpy as np
        HEADS = 16
        MASK_VAL = 1000000000000.0
        key = jax.random.key(seed)
        ks = jax.random.split(key, 6)
        B, S, F = (2, 256, 128)
        scale = 1.0 / np.sqrt(F)
        return {'attend_from': jax.random.normal(ks[0], (B, S, F), jnp.float32), 'attend_to': jax.random.normal(ks[1], (B, S, F), jnp.float32), 'w_q': jax.random.normal(ks[2], (F, F), jnp.float32) * scale, 'b_q': jnp.zeros((F,), jnp.float32), 'w_kv': jax.random.normal(ks[3], (F, 2 * F), jnp.float32) * scale, 'b_kv': jnp.zeros((2 * F,), jnp.float32), 'w_out': jax.random.normal(ks[4], (F, F), jnp.float32) * scale, 'b_out': jnp.zeros((F,), jnp.float32)}
    _L0_xattn_all = _L0_xattn_setup()
    _L0_xattn_in = {k: v for k, v in _L0_xattn_all.items() if k in ('w_q', 'b_q', 'w_kv', 'b_kv', 'w_out', 'b_out')}
    del _L0_xattn_all

    def _L0_ffn_setup():
        import jax, jax.numpy as jnp
        import numpy as np
        from jax import lax
        D = 128
        H = 176
        E = 8
        K = 2
        ROUTER_SCALE = 1.0

        def _expert(x, w1, b1, w3, b3, w2, b2):
            h = jax.nn.silu((x @ w1 + b1) * (x @ w3 + b3))
            return h @ w2 + b2
        key = jax.random.key(seed)
        ks = jax.random.split(key, 16)
        s = 0.02
        inp = {'x': jax.random.normal(ks[0], (2, 256, D), dtype=jnp.float32), 'gate_w': jax.random.normal(ks[1], (E, D), dtype=jnp.float32) * s, 'gate_b': jax.random.normal(ks[2], (E,), dtype=jnp.float32) * s, 'w1': jax.random.normal(ks[3], (E, D, H), dtype=jnp.float32) * s, 'b1': jax.random.normal(ks[4], (E, H), dtype=jnp.float32) * s, 'w3': jax.random.normal(ks[5], (E, D, H), dtype=jnp.float32) * s, 'b3': jax.random.normal(ks[6], (E, H), dtype=jnp.float32) * s, 'w2': jax.random.normal(ks[7], (E, H, D), dtype=jnp.float32) * s, 'b2': jax.random.normal(ks[8], (E, D), dtype=jnp.float32) * s, 'sw1': jax.random.normal(ks[9], (D, H), dtype=jnp.float32) * s, 'sb1': jax.random.normal(ks[10], (H,), dtype=jnp.float32) * s, 'sw3': jax.random.normal(ks[11], (D, H), dtype=jnp.float32) * s, 'sb3': jax.random.normal(ks[12], (H,), dtype=jnp.float32) * s, 'sw2': jax.random.normal(ks[13], (H, D), dtype=jnp.float32) * s, 'sb2': jax.random.normal(ks[14], (D,), dtype=jnp.float32) * s}
        return inp
    _L0_ffn_all = _L0_ffn_setup()
    _L0_ffn_in = {k: v for k, v in _L0_ffn_all.items() if k in ('gate_w', 'gate_b', 'w1', 'b1', 'w3', 'b3', 'w2', 'b2', 'sw1', 'sb1', 'sw3', 'sb3', 'sw2', 'sb2')}
    del _L0_ffn_all
    return {'x': x, 'ctx_1024': ctx_1024, 'L0_xattn_w_q': _L0_xattn_in['w_q'], 'L0_xattn_b_q': _L0_xattn_in['b_q'], 'L0_xattn_w_kv': _L0_xattn_in['w_kv'], 'L0_xattn_b_kv': _L0_xattn_in['b_kv'], 'L0_xattn_w_out': _L0_xattn_in['w_out'], 'L0_xattn_b_out': _L0_xattn_in['b_out'], 'L0_ffn_gate_w': _L0_ffn_in['gate_w'], 'L0_ffn_gate_b': _L0_ffn_in['gate_b'], 'L0_ffn_w1': _L0_ffn_in['w1'], 'L0_ffn_b1': _L0_ffn_in['b1'], 'L0_ffn_w3': _L0_ffn_in['w3'], 'L0_ffn_b3': _L0_ffn_in['b3'], 'L0_ffn_w2': _L0_ffn_in['w2'], 'L0_ffn_b2': _L0_ffn_in['b2'], 'L0_ffn_sw1': _L0_ffn_in['sw1'], 'L0_ffn_sb1': _L0_ffn_in['sb1'], 'L0_ffn_sw3': _L0_ffn_in['sw3'], 'L0_ffn_sb3': _L0_ffn_in['sb3'], 'L0_ffn_sw2': _L0_ffn_in['sw2'], 'L0_ffn_sb2': _L0_ffn_in['sb2']}

def reference(x, ctx_1024, L0_xattn_w_q, L0_xattn_b_q, L0_xattn_w_kv, L0_xattn_b_kv, L0_xattn_w_out, L0_xattn_b_out, L0_ffn_gate_w, L0_ffn_gate_b, L0_ffn_w1, L0_ffn_b1, L0_ffn_w3, L0_ffn_b3, L0_ffn_w2, L0_ffn_b2, L0_ffn_sw1, L0_ffn_sb1, L0_ffn_sw3, L0_ffn_sb3, L0_ffn_sw2, L0_ffn_sb2):
    import jax
    import jax.numpy as jnp

    def _L0_xattn_ref(attend_from, attend_to, w_q, b_q, w_kv, b_kv, w_out, b_out):
        import jax, jax.numpy as jnp
        import numpy as np
        HEADS = 16
        MASK_VAL = 1000000000000.0
        B, S, F = attend_from.shape
        H = HEADS
        d = F // H
        Z = attend_to.shape[1]
        qry = (attend_from @ w_q + b_q).reshape(B, S, H, d)
        kv = attend_to @ w_kv + b_kv
        key, val = jnp.split(kv, 2, axis=-1)
        key = key.reshape(B, Z, H, d)
        val = val.reshape(B, Z, H, d)
        logits = jnp.einsum('bshd,bzhd->bhsz', qry, key)
        mask = jnp.triu(jnp.ones((S, Z), dtype=logits.dtype)) * MASK_VAL
        logits = logits - mask
        attn = jax.nn.softmax(logits, axis=-1)
        out = jnp.einsum('bhsz,bzhd->bshd', attn, val).reshape(B, S, F)
        return out @ w_out + b_out

    def _L0_ffn_ref(x, gate_w, gate_b, w1, b1, w3, b3, w2, b2, sw1, sb1, sw3, sb3, sw2, sb2):
        import jax, jax.numpy as jnp
        import numpy as np
        from jax import lax
        D = 128
        H = 176
        E = 8
        K = 2
        ROUTER_SCALE = 1.0

        def _expert(x, w1, b1, w3, b3, w2, b2):
            h = jax.nn.silu((x @ w1 + b1) * (x @ w3 + b3))
            return h @ w2 + b2
        shape = x.shape
        xf = x.reshape(-1, D)
        T = xf.shape[0]
        scores = jax.nn.softmax(xf @ gate_w.T, axis=-1)
        biased = scores + gate_b
        _, idx = lax.top_k(biased, K)
        w = jnp.take_along_axis(scores, idx, axis=-1) * ROUTER_SCALE
        rw = jnp.zeros((T, E), dtype=xf.dtype).at[jnp.arange(T)[:, None], idx].add(w)
        h = jax.nn.silu((jnp.einsum('td,edh->teh', xf, w1) + b1) * (jnp.einsum('td,edh->teh', xf, w3) + b3))
        oe = jnp.einsum('teh,ehd->ted', h, w2) + b2
        y = jnp.einsum('te,ted->td', rw, oe)
        z = _expert(xf, sw1, sb1, sw3, sb3, sw2, sb2)
        return (y + z).reshape(shape)
    x = x + _L0_xattn_ref(_layernorm(x, axis=-1), ctx_1024, L0_xattn_w_q, L0_xattn_b_q, L0_xattn_w_kv, L0_xattn_b_kv, L0_xattn_w_out, L0_xattn_b_out)
    x = x + _L0_ffn_ref(_layernorm(x, axis=-1), L0_ffn_gate_w, L0_ffn_gate_b, L0_ffn_w1, L0_ffn_b1, L0_ffn_w3, L0_ffn_b3, L0_ffn_w2, L0_ffn_b2, L0_ffn_sw1, L0_ffn_sb1, L0_ffn_sw3, L0_ffn_sb3, L0_ffn_sw2, L0_ffn_sb2)
    return x

_drawn_inputs = setup_inputs


def setup_inputs(seed=0):
    import zlib

    import numpy as np

    out = dict(_drawn_inputs(seed))
    spreads = {'L0_xattn_b_q': (0.0, 0.1), 'L0_xattn_b_kv': (0.0, 0.1), 'L0_xattn_b_out': (0.0, 0.1)}
    factors = {'L0_ffn_gate_w': 8.0,
     'L0_ffn_gate_b': 8.0,
     'L0_ffn_w1': 8.0,
     'L0_ffn_b1': 8.0,
     'L0_ffn_w3': 8.0,
     'L0_ffn_b3': 8.0,
     'L0_ffn_w2': 8.0,
     'L0_ffn_b2': 29.239,
     'L0_ffn_sw1': 8.0,
     'L0_ffn_sb1': 8.0,
     'L0_ffn_sw3': 8.0,
     'L0_ffn_sb3': 8.0,
     'L0_ffn_sw2': 8.0,
     'L0_ffn_sb2': 16.837}
    for name, (base, spread) in spreads.items():
        noise = np.random.default_rng([zlib.crc32(name.encode()), seed]).standard_normal(out[name].shape)
        drawn = base * np.exp(spread * noise) if base else spread * noise
        out[name] = jnp.asarray(drawn.astype(out[name].dtype))
    for name, factor in factors.items():
        out[name] = (out[name] * factor).astype(out[name].dtype)
    return out
```

```python
from contextlib import ExitStack

import concourse.bass as bass
from concourse import mybir
from concourse.alu_op_type import AluOpType as ALU

B, S, D, Z = 4, 512, 128, 77
HEADS, HD = 16, 8
E, HID = 8, 176
P = 128
NT = S // P
HZ = HEADS * Z
NZC = -(-HZ // P)
HZP = NZC * P
HALF = HZ // 2
QUART = HZ // 4
VC = HD + 1
VW_W = HEADS * VC
WIN_HEADS = 11
NFC = -(-(E + 1) * HID // P)
NEC = E * HID // P
FP = NFC * P
BANK = 512
EPS = 1e-5
MASK = 1e12
GW = 96
REP = 3 * Z
CHUNKS = list(range(NEC, NFC)) + list(range(NEC))
assert NEC * P == E * HID

C_ID, C_HM, C_TRI, C_ZM, C_LT = 0, P, P + HEADS, P + HEADS + Z, P + HEADS + Z + NZC * HEADS
C_END = C_LT + E * E
V_BQ, V_BK, V_BV, V_B1, V_B3 = 0, 1, 2, 3, 3 + NFC
V_BO = V_B3 + NFC
V_GB = V_BO + D
V_END = V_GB + E


def build(nc, x, ctx_t, ctx_rep, w_q, w_kv, w_out, gate_wt, w1, w3, w2, b2, vecs, consts, sel_rows, out):
    f32, f32r = mybir.dt.float32, mybir.dt.float32r
    ACT = mybir.ActivationFunctionType
    AX = mybir.AxisListType.X

    st = ExitStack()
    with st:
        def sb(name, cols, dt=f32):
            return st.enter_context(nc.sbuf_tensor(name, [P, cols], dt))

        def bank(name, n=1):
            return st.enter_context(nc.psum_tensor(name, [P, n * BANK], f32))

        def sem(name):
            return st.enter_context(nc.semaphore(name))

        x_all = sb("x_all", B * S)
        xb_all = sb("xb_all", B * S)
        ctx_sb = sb("ctx_sb", B * Z)
        rep_all = sb("rep_all", B * REP)
        rep_cur = sb("rep_cur", REP)
        wq_sb = sb("wq_sb", D)
        wkv_sb = sb("wkv_sb", 2 * D)
        wo_sb = sb("wo_sb", D)
        gw_sb = sb("gw_sb", GW)
        cst = sb("cst", C_END)
        vec = sb("vec", V_END)
        w1_sb, w3_sb, w2_sb = sb("w1_sb", FP), sb("w3_sb", FP), sb("w2_sb", FP)
        b2_sb = sb("b2_sb", D)
        sel_sb = sb("sel_sb", NEC * P)
        wq_hi, wq_lo = sb("wq_hi", D, f32r), sb("wq_lo", D, f32r)
        gw_hi, gw_lo = sb("gw_hi", GW, f32r), sb("gw_lo", GW, f32r)
        w1_hi, w1_lo = sb("w1_hi", FP, f32r), sb("w1_lo", FP, f32r)
        w3_hi, w3_lo = sb("w3_hi", FP, f32r), sb("w3_lo", FP, f32r)
        w2_hi, w2_lo = sb("w2_hi", FP, f32r), sb("w2_lo", FP, f32r)
        b2_st = sb("b2_st", D, f32r)
        sel = sb("sel", NEC * P, f32r)
        k_f = sb("k_f", B * Z)
        k_hi, k_lo = sb("k_hi", B * Z, f32r), sb("k_lo", B * Z, f32r)
        kb_hi, kb_lo = sb("kb_hi", HZ, f32r), sb("kb_lo", HZ, f32r)
        vw = sb("vw", NZC * VW_W)
        stats = sb("stats", NT * 6)
        mv = sb("mv", NT * 2)
        veps = sb("veps", NT)
        rstd = sb("rstd", NT)
        mhalf = sb("mhalf", NT)
        spare = sb("spare", 1)
        xn = sb("xn", S)
        xt_hi, xt_lo = sb("xt_hi", S, f32r), sb("xt_lo", S, f32r)
        q_hi, q_lo = sb("q_hi", S, f32r), sb("q_lo", S, f32r)
        lg = [sb(f"lg{i}", HZP) for i in range(2)]
        mx = sb("mx", 2 * HEADS)
        pt = [sb(f"pt{i}", HZP) for i in range(2)]
        rden = sb("rden", 2 * HEADS)
        ao = sb("ao", S)
        aot = sb("aot", S)
        x1 = sb("x1", S)
        x2t_hi, x2t_lo = sb("x2t_hi", S, f32r), sb("x2t_lo", S, f32r)
        gmax, gsum, grec = sb("gmax", NT), sb("gsum", NT), sb("grec", NT)
        ge, gs, gbias = sb("ge", NT * E), sb("gs", NT * E), sb("gbias", NT * E)
        cgt, ceq = sb("cgt", NT * E * E), sb("ceq", NT * E * E)
        rank, chosen = sb("rank", NT * E), sb("chosen", NT * E)
        rw = sb("rw", NT * P)
        rwt = sb("rwt", S, f32r)
        u_sb = [sb(f"u_sb{i}", S) for i in range(2)]
        p_sb = [sb(f"p_sb{i}", S) for i in range(2)]
        s_sb = [sb(f"s_sb{i}", S) for i in range(2)]
        h_sb = [sb(f"h_sb{i}", S) for i in range(3)]
        h_hi = [sb(f"h_hi{i}", S, f32r) for i in range(3)]
        h_lo = [sb(f"h_lo{i}", S, f32r) for i in range(3)]
        y_sb = sb("y_sb", S)

        ps03 = bank("ps03", 4)
        ps45 = bank("ps45", 2)
        ps6 = bank("ps6")
        ps7 = bank("ps7")

        def lg_ps(half, q4):
            o = (2 * half + q4) * BANK
            return ps03[:, o:o + QUART]

        def lg_half(half):
            return ps03[:, 2 * half * BANK:(2 * half + 2) * BANK].rearrange("p (a n) -> p a n", a=2)[:, :, 0:QUART] \
                .rearrange("p a (h z) -> p a h z", z=Z)

        def pair(i):
            return ps45[:, i * BANK:(i + 1) * BANK]

        def u_ps(i):
            return ps03[:, i * BANK:(i + 1) * BANK]

        def v_ps(i):
            return ps03[:, (2 + i) * BANK:(3 + i) * BANK]

        ident = cst[:, C_ID:C_ID + P]
        bq, bk, bv = (vec[:, v:v + 1] for v in (V_BQ, V_BK, V_BV))
        vw4 = vw[:, :].rearrange("p (c h v) -> p c h v", c=NZC, h=HEADS)
        rw3 = rw[:, :].rearrange("p (t n) -> p t n", t=NT)

        def tile_of(ap, t):
            return ap[:, t * P:(t + 1) * P]

        x_in = sem("x_in")
        attn_in = sem("attn_in")
        ffn_in = sem("ffn_in")
        out_done = sem("out_done")
        pads = sem("pads")
        dve_pads = sem("dve_pads")
        wq_split = sem("wq_split")
        k_proj, k_bias, k_split = sem("k_proj"), sem("k_bias"), sem("k_split")
        xb_ready = sem("xb_ready")
        w_his, w_split = sem("w_his"), sem("w_split")
        kb_ready = sem("kb_ready")
        rep_ready = sem("rep_ready")
        vp_ready, vw_ready = sem("vp_ready"), sem("vw_ready")
        st_ready, mv_ready, ve_ready, rstd_ready, xn_ready = (sem(n) for n in ("st_ready", "mv_ready", "ve_ready", "rstd_ready", "xn_ready"))
        xt_ps_ready, xt_hi_ready, xt_lo_ready = sem("xt_ps_ready"), sem("xt_hi_ready"), sem("xt_lo_ready")
        q_ps_ready, q_hi_ready, q_lo_ready = sem("q_ps_ready"), sem("q_hi_ready"), sem("q_lo_ready")
        lg_ready, lg_masked, mx_ready, lg_sub, exp_done = (sem(n) for n in ("lg_ready", "lg_masked", "mx_ready", "lg_sub", "exp_done"))
        pt_ps_ready, pt_moved = sem("pt_ps_ready"), sem("pt_moved")
        av_ready, rden_ready, ao_ready = sem("av_ready"), sem("rden_ready"), sem("ao_ready")
        aot_ps_ready, aot_ready, proj_ready, x1_ready = (sem(n) for n in ("aot_ps_ready", "aot_ready", "proj_ready", "x1_ready"))
        x2_ps_ready, x2_hi_ready, x2_lo_ready = sem("x2_ps_ready"), sem("x2_hi_ready"), sem("x2_lo_ready")
        gate_ready, gchain, gexp_ready, gsub_ready = sem("gate_ready"), sem("gchain"), sem("gexp_ready"), sem("gsub_ready")
        rw_ready, rwt_ps_ready, rwt_hi_ready, rwt_ready = (sem(n) for n in ("rw_ready", "rwt_ps_ready", "rwt_hi_ready", "rwt_ready"))
        u_ready, u_moved, v_ready, p_ready = sem("u_ready"), sem("u_moved"), sem("v_ready"), sem("p_ready")
        s_ready, rb_ready, h_ready = sem("s_ready"), sem("rb_ready"), sem("h_ready")
        h_hi_ready, h_lo_ready, down_done = sem("h_hi_ready"), sem("h_lo_ready"), sem("down_done")
        y_ready, y_moved = sem("y_ready"), sem("y_moved")

        N_ATTN_IN, N_FFN_IN, N_PADS = 7, 10, 13

        block = st.enter_context(nc.Block())

        @block.sync
        def _(sp):
            sp.dma_start(x_all[:, :].rearrange("p (b n) -> p b n", b=B), x.rearrange("b p n -> p b n")).then_inc(x_in, 16)
            sp.dma_start(cst[:, :], consts).then_inc(attn_in, 16)
            sp.dma_start(wq_sb[:, :], w_q).then_inc(attn_in, 16)
            sp.dma_start(ctx_sb[:, :], ctx_t).then_inc(attn_in, 16)
            sp.dma_start(wkv_sb[:, :], w_kv).then_inc(attn_in, 16)
            sp.dma_start(vec[:, :], vecs).then_inc(attn_in, 16)
            sp.dma_start(rep_all[:, :], ctx_rep).then_inc(attn_in, 16)
            sp.dma_start(wo_sb[:, :], w_out).then_inc(attn_in, 16)
            sp.dma_start(w1_sb[:, 0:(E + 1) * HID], w1).then_inc(ffn_in, 16)
            sp.dma_start(w3_sb[:, 0:(E + 1) * HID], w3).then_inc(ffn_in, 16)
            sp.dma_start(w2_sb[:, 0:NEC * P + D], w2[:, 0:NEC * P + D]).then_inc(ffn_in, 16)
            last = (E + 1) * HID - (NFC - 1) * P
            sp.wait_ge(pads, 4)
            sp.dma_start(w2_sb[0:last, FP - D:FP], w2[0:last, FP - D:FP]).then_inc(ffn_in, 16)
            sp.dma_start(gw_sb[:, 0:E], gate_wt).then_inc(ffn_in, 16)
            for q in range(3):
                sp.dma_start(b2_sb[32 * q:32 * q + E + 1, :], b2).then_inc(ffn_in, 16)
            for q in range(2):
                sp.dma_start(sel_sb[32 * q:32 * q + E, :], sel_rows).then_inc(ffn_in, 16)
            with sp.Fori(0, B) as b:
                sp.wait_ge(y_moved, b + 2)
                sp.dma_start(out[b, :, :], y_sb[:, :]).then_inc(out_done, 16)
            sp.wait_ge(out_done, 16 * (B + 1))

        @block.gpsimd
        def _(pool):
            pool.memset(w2_sb[:, FP - D:FP], 0.0).then_inc(pads, 1)
            pool.memset(gw_sb[:, :], 0.0).then_inc(pads, 1)
            pool.memset(b2_sb[:, :], 0.0).then_inc(pads, 1)
            pool.memset(sel_sb[:, :], 0.0).then_inc(pads, 1)
            pool.memset(w1_sb[:, (E + 1) * HID:FP], 0.0).then_inc(pads, 1)
            pool.memset(w3_sb[:, (E + 1) * HID:FP], 0.0).then_inc(pads, 1)
            for i in range(2):
                pool.memset(lg[i][:, HZ:HZP], 0.0).then_inc(pads, 1)
            pool.memset(rw[:, :], 0.0).then_inc(pads, 1)
            pool.memset(mhalf[:, :], -0.5).then_inc(pads, 1)
            pool.wait_ge(pads, 10)
            for q in range(3):
                pool.memset(rw3[:, :, 32 * q + E:32 * q + E + 1], 1.0).then_inc(pads, 1)
            pool.wait_ge(x_in, 16)
            pool.wait_ge(attn_in, 16 * N_ATTN_IN)

            def rstd_step(k):
                pool.wait_ge(ve_ready, k + 1)
                pool.tensor_tensor(rstd[:, :], veps[:, :], mhalf[:, :], ALU.pow).then_inc(rstd_ready, 1)

            def batch(b):
                rstd_step(2 * b)
                pool.wait_ge(mx_ready, 2 * NT * b + 1)
                for kb, k in ((kb_hi, k_hi), (kb_lo, k_lo)):
                    keys = k[:, bass.ts(b, Z)].bitcast(f32)
                    pool.tensor_tensor(kb[:, :].rearrange("p (h z) -> p h z", h=HEADS),
                                       keys.unsqueeze(1).broadcast_to([P, HEADS, Z]),
                                       cst[:, C_HM:C_HM + HEADS].unsqueeze(2).broadcast_to([P, HEADS, Z]),
                                       ALU.mult).then_inc(kb_ready, 1)
                pool.wait_ge(vw_ready, 3 * b + 1)
                pool.tensor_copy(rep_cur[:, :], rep_all[:, bass.ts(b, REP)]).then_inc(rep_ready, 1)
                rstd_step(2 * b + 1)
                for n, c in enumerate(CHUNKS):
                    k = b * NFC + n
                    pool.wait_ge(h_hi_ready, k + 1)
                    pool.wait_ge(down_done, k + 1)
                    pool.tensor_tensor(h_lo[n % 3][:, :], h_sb[n % 3][:, :], h_hi[n % 3][:, :].bitcast(f32),
                                       ALU.subtract).then_inc(h_lo_ready, 1)

            pool.tensor_tensor(xb_all[:, :].rearrange("p (t d) -> p t d", d=D),
                               x_all[:, :].rearrange("p (t d) -> p t d", d=D),
                               vec[:, V_BO:V_BO + D].unsqueeze(1).broadcast_to([P, B * NT, D]),
                               ALU.add).then_inc(xb_ready, 1)
            pool.wait_ge(w_his, 6)
            third = slice(64, 96)
            pool.wait_ge(xb_ready, 1)
            pool.tensor_tensor(b2_st[third, :], b2_sb[third, :], b2_st[third, :].bitcast(f32), ALU.subtract).then_inc(w_split, 1)
            pool.wait_ge(w_split, 1)
            for lo, w, hi in ((gw_lo[:, :], gw_sb[:, :], gw_hi[:, :]), (w1_lo[:, :], w1_sb[:, :], w1_hi[:, :]),
                              (w3_lo[:, :], w3_sb[:, :], w3_hi[:, :]), (w2_lo[:, :], w2_sb[:, :], w2_hi[:, :])):
                pool.tensor_tensor(lo, w, hi.bitcast(f32), ALU.subtract).then_inc(w_split, 1)
            pool.wait_ge(k_split, 2)
            with pool.Fori(0, B) as b:
                batch(b)

        @block.scalar
        def _(act):
            act.sem_inc(pt_moved, 2)
            act.sem_inc(u_moved, 2)
            act.sem_inc(y_moved, 1)
            act.sem_inc(out_done, 16)
            act.wait_ge(k_proj, 1)
            act.activation(k_f[:, :], ps7[:, 0:B * Z], ACT.Identity, bias=bk).then_inc(k_bias, 1)
            act.wait_ge(ffn_in, 16 * N_FFN_IN)
            act.wait_ge(pads, N_PADS)
            for hi, w in ((w1_hi, w1_sb), (w3_hi, w3_sb), (w2_hi, w2_sb), (gw_hi, gw_sb), (b2_st, b2_sb), (sel, sel_sb)):
                act.activation(hi[:, :], w[:, :], ACT.Copy).then_inc(w_his, 1)

            def batch(b):
                act.wait_ge(xt_ps_ready, b + 1)
                act.activation(xt_hi[:, :], ps7[:, :], ACT.Copy).then_inc(xt_hi_ready, 1)
                act.wait_ge(q_ps_ready, b + 1)
                act.activation(q_hi[:, :], ps6[:, :], ACT.Identity, bias=bq).then_inc(q_hi_ready, 1)

                def exps(half):
                    t, g = divmod(half, 2)
                    part = lg[t % 2][:, g * HALF:(g + 1) * HALF]
                    act.wait_ge(lg_sub, b * 2 * NT + half + 3)
                    act.activation(part, part, ACT.Exp).then_inc(exp_done, 1)

                def move_pt(t):
                    for g in range(3):
                        k = b * 3 * NT + 3 * t + g
                        cols = min(BANK, HZP - g * BANK)
                        act.wait_ge(pt_ps_ready, k + 1)
                        if t >= 2 and g == 0:
                            act.wait_ge(av_ready, b * NT + t - 1)
                        act.activation(pt[t % 2][:, g * BANK:g * BANK + cols], pair(k_of(t, g) % 2)[:, 0:cols],
                                       ACT.Copy).then_inc(pt_moved, 1)

                def k_of(t, g):
                    return 3 * t + g

                for t in range(NT):
                    exps(2 * t)
                    exps(2 * t + 1)
                    if t >= 1:
                        move_pt(t - 1)
                move_pt(NT - 1)
                act.wait_ge(aot_ps_ready, b + 1)
                act.activation(aot[:, :], ps7[:, :], ACT.Identity, bias=bv).then_inc(aot_ready, 1)
                act.wait_ge(x2_ps_ready, b + 1)
                act.activation(x2t_hi[:, :], ps7[:, :], ACT.Copy).then_inc(x2_hi_ready, 1)
                act.wait_ge(gsub_ready, b + 1)
                act.activation(ge[:, :], ge[:, :], ACT.Exp).then_inc(gexp_ready, 1)

                def u_step(n):
                    k = b * NFC + n
                    c = CHUNKS[n]
                    act.wait_ge(u_ready, k + 1)
                    act.wait_ge(p_ready, k + 1)
                    act.activation(u_sb[n % 2][:, :], u_ps(n % 2), ACT.Identity,
                                   bias=vec[:, V_B1 + c:V_B1 + c + 1]).then_inc(u_moved, 1)

                def silu_step(n):
                    k = b * NFC + n
                    act.wait_ge(p_ready, k + 3)
                    act.wait_ge(h_lo_ready, k + 1)
                    dst = h_sb[n % 3] if CHUNKS[n] >= NEC else s_sb[n % 2]
                    act.activation(dst[:, :], p_sb[n % 2][:, :], ACT.Silu).then_inc(s_ready, 1)

                def hi_step(n):
                    k = b * NFC + n
                    if CHUNKS[n] < NEC:
                        act.wait_ge(h_ready, b * NEC + (n - (NFC - NEC)) + 1)
                    else:
                        act.wait_ge(s_ready, k + 1)
                    act.wait_ge(down_done, k + 1)
                    act.activation(h_hi[n % 3][:, :], h_sb[n % 3][:, :], ACT.Copy).then_inc(h_hi_ready, 1)

                def late(n):
                    if n == 2:
                        act.wait_ge(rwt_ps_ready, b + 1)
                        act.activation(rwt[:, :], ps7[:, :], ACT.Copy).then_inc(rwt_hi_ready, 1)

                for n in range(NFC + 2):
                    late(n)
                    if n < NFC:
                        u_step(n)
                    if 1 <= n <= NFC:
                        silu_step(n - 1)
                    if n >= 2:
                        hi_step(n - 2)
                act.wait_ge(y_ready, b + 1)
                act.wait_ge(out_done, 16 * b + 16)
                act.activation(y_sb[:, :], ps6[:, :], ACT.Copy).then_inc(y_moved, 1)

            with act.Fori(0, B) as b:
                batch(b)

        @block.vector
        def _(dve):
            dve.sem_inc(lg_sub, 2)
            dve.sem_inc(mx_ready, 1)
            dve.sem_inc(vw_ready, 1)
            dve.sem_inc(p_ready, 2)
            dve.sem_inc(down_done, 3)
            dve.sem_inc(h_lo_ready, 3)
            dve.wait_ge(attn_in, 16 * N_ATTN_IN)
            dve.wait_ge(pads, N_PADS)
            dve.wait_ge(x_in, 16)
            dve.tensor_copy(wq_hi[:, :], wq_sb[:, :]).then_inc(wq_split, 1)
            dve.wait_ge(wq_split, 1)
            dve.tensor_tensor(wq_lo[:, :], wq_sb[:, :], wq_hi[:, :].bitcast(f32), ALU.subtract).then_inc(wq_split, 1)
            dve.tensor_copy(vw4[:, :, :, HD], cst[:, C_ZM:C_ZM + NZC * HEADS].rearrange("p (c h) -> p c h", c=NZC)) \
                .then_inc(dve_pads, 1)
            dve.wait_ge(k_bias, 1)
            dve.tensor_copy(k_hi[:, :], k_f[:, :]).then_inc(k_split, 1)
            dve.wait_ge(k_split, 1)
            dve.tensor_tensor(k_lo[:, :], k_f[:, :], k_hi[:, :].bitcast(f32), ALU.subtract).then_inc(k_split, 1)

            def layer_norm(k, src, src_tile):
                for t in range(NT):
                    dve.bn_stats(stats[:, 6 * t:6 * t + 6], src_tile(t)).then_inc(st_ready, 1)
                dve.wait_ge(st_ready, k * NT + NT)
                dve.memset(spare[:, :], 0.0)
                for t in range(NT):
                    dve.bn_aggr(mv[:, 2 * t:2 * t + 2], stats[:, 6 * t:6 * t + 6]).then_inc(mv_ready, 1)
                dve.wait_ge(mv_ready, k * NT + NT)
                dve.tensor_scalar(veps[:, :], mv[:, :].rearrange("p (t s) -> p t s", s=2)[:, :, 1], EPS, None,
                                  ALU.add).then_inc(ve_ready, 1)
                dve.wait_ge(rstd_ready, k + 1)
                for t in range(NT):
                    dve.tensor_scalar(tile_of(xn, t), src_tile(t), mv[:, 2 * t:2 * t + 1], rstd[:, t:t + 1],
                                      ALU.subtract, ALU.mult).then_inc(xn_ready, 1)

            def batch(b):
                layer_norm(2 * b, None, lambda t: x_all[:, bass.ds(b * S + t * P, P)])
                dve.wait_ge(xt_hi_ready, b + 1)
                dve.tensor_tensor(xt_lo[:, :], ps7[:, :], xt_hi[:, :].bitcast(f32), ALU.subtract).then_inc(xt_lo_ready, 1)
                dve.wait_ge(q_hi_ready, b + 1)
                dve.scalar_tensor_tensor(q_lo[:, :], ps6[:, :], bq, q_hi[:, :].bitcast(f32),
                                         ALU.add, ALU.subtract).then_inc(q_lo_ready, 1)
                for g in range(3):
                    c0, n = 4 * g, min(4, NZC - 4 * g)
                    dve.wait_ge(vp_ready, 3 * b + g + 1)
                    dve.tensor_tensor(vw4[:, c0:c0 + n, :, 0:HD],
                                      (ps7 if g % 2 == 0 else ps6)[:, 0:n * P].rearrange("p (c h v) -> p c h v", c=n, v=HD),
                                      cst[:, C_ZM + c0 * HEADS:C_ZM + (c0 + n) * HEADS]
                                      .rearrange("p (c h) -> p c h", c=n).unsqueeze(3).broadcast_to([P, n, HEADS, HD]),
                                      ALU.mult).then_inc(vw_ready, 1)

                def logits_half(half):
                    t, g = divmod(half, 2)
                    k = b * 2 * NT + half
                    dst = lg[t % 2][:, g * HALF:(g + 1) * HALF].rearrange("p (a h z) -> p a h z", a=2, z=Z)
                    m = mx[:, g * 8:g * 8 + 8]
                    src = lg_half(half % 2)
                    dve.wait_ge(lg_ready, k + 1)
                    if half >= 4:
                        dve.wait_ge(pt_ps_ready, b * 3 * NT + 3 * (t - 1))
                    if t == 0:
                        for a in range(2):
                            dve.tensor_tensor(dst[:, a], src[:, a],
                                              cst[:, C_TRI:C_TRI + Z].unsqueeze(1).broadcast_to([P, 4, Z]),
                                              ALU.subtract).then_inc(lg_masked, 1)
                        src = dst
                        dve.wait_ge(lg_masked, 4 * b + 2 * g + 2)
                    dve.tensor_reduce(m.rearrange("p (a h) -> p a h", a=2), src, AX, ALU.max).then_inc(mx_ready, 1)
                    dve.wait_ge(mx_ready, k + 2)
                    dve.tensor_tensor(dst, src, m.rearrange("p (a h) -> p a h", a=2).unsqueeze(3).broadcast_to([P, 2, 4, Z]),
                                      ALU.subtract).then_inc(lg_sub, 1)

                def normalise(pr):
                    src = ps6[:, 0:2 * VW_W].rearrange("p (t h v) -> p t h v", t=2, v=VC)
                    dve.wait_ge(av_ready, b * NT + 2 * pr + 2)
                    dve.reciprocal(rden[:, :].rearrange("p (t h) -> p t h", t=2), src[:, :, :, HD]).then_inc(rden_ready, 1)
                    dve.wait_ge(rden_ready, 2 * b + pr + 1)
                    dve.tensor_tensor(ao[:, 2 * pr * P:2 * (pr + 1) * P].rearrange("p (t h v) -> p t h v", t=2, v=HD),
                                      src[:, :, :, 0:HD],
                                      rden[:, :].rearrange("p (t h) -> p t h", t=2).unsqueeze(3).broadcast_to([P, 2, HEADS, HD]),
                                      ALU.mult).then_inc(ao_ready, 1)

                for half in range(2 * NT):
                    logits_half(half)
                normalise(0)
                normalise(1)
                dve.wait_ge(proj_ready, b + 1)
                dve.wait_ge(xb_ready, 1)
                dve.tensor_tensor(x1[:, :], ps6[:, :], xb_all[:, bass.ts(b, S)], ALU.add).then_inc(x1_ready, 1)
                dve.wait_ge(x1_ready, b + 1)
                layer_norm(2 * b + 1, None, lambda t: tile_of(x1, t))
                dve.wait_ge(x2_hi_ready, b + 1)
                dve.tensor_tensor(x2t_lo[:, :], ps7[:, :], x2t_hi[:, :].bitcast(f32), ALU.subtract).then_inc(x2_lo_ready, 1)

                links = 11
                step = [0]

                def link(ins):
                    step[0] += 1
                    ins.then_inc(gchain, 1)
                    dve.wait_ge(gchain, b * links + step[0])

                def per_token(ap):
                    return ap[:, :].unsqueeze(2).broadcast_to([P, NT, E])

                def tok(ap):
                    return ap[:, :].rearrange("p (t e) -> p t e", t=NT)

                def router_a():
                    scores = ps6[:, 0:NT * GW].rearrange("p (t n) -> p t n", t=NT)[:, :, 0:E]
                    dve.wait_ge(gate_ready, b + 1)
                    link(dve.tensor_reduce(gmax[:, :], scores, AX, ALU.max))
                    dve.tensor_tensor(tok(ge), scores, per_token(gmax), ALU.subtract).then_inc(gsub_ready, 1)

                def router_b():
                    dve.wait_ge(gexp_ready, b + 1)
                    link(dve.tensor_reduce(gsum[:, :], tok(ge), AX, ALU.add))
                    link(dve.reciprocal(grec[:, :], gsum[:, :]))
                    link(dve.tensor_tensor(tok(gs), tok(ge), per_token(grec), ALU.mult))
                    link(dve.tensor_tensor(tok(gbias), tok(gs),
                                           vec[:, V_GB:V_GB + E].unsqueeze(1).broadcast_to([P, NT, E]), ALU.add))
                    pairs = [P, NT * E, E]
                    gt = cgt[:, :].rearrange("p (n f) -> p n f", f=E)
                    eq = ceq[:, :].rearrange("p (n f) -> p n f", f=E)
                    for t in range(NT):
                        mine = gbias[:, t * E:(t + 1) * E].unsqueeze(2).broadcast_to([P, E, E])
                        others = gbias[:, t * E:(t + 1) * E].unsqueeze(1).broadcast_to([P, E, E])
                        dve.tensor_tensor(gt[:, t * E:(t + 1) * E, :], others, mine, ALU.is_gt)
                        last = dve.tensor_tensor(eq[:, t * E:(t + 1) * E, :], others, mine, ALU.is_equal)
                    link(last)
                    link(dve.tensor_tensor(ceq[:, :].rearrange("p (t n) -> p t n", t=NT), ceq[:, :].rearrange("p (t n) -> p t n", t=NT),
                                           cst[:, C_LT:C_LT + E * E].unsqueeze(1).broadcast_to([P, NT, E * E]), ALU.mult))
                    link(dve.tensor_tensor(cgt[:, :], cgt[:, :], ceq[:, :], ALU.add))
                    link(dve.tensor_reduce(rank[:, :], gt, AX, ALU.add))
                    link(dve.tensor_scalar(chosen[:, :], rank[:, :], 2.0, None, ALU.is_lt))
                    link(dve.tensor_tensor(tok(gs), tok(gs), tok(chosen), ALU.mult))
                    for q in range(3):
                        last = dve.tensor_copy(rw3[:, :, 32 * q:32 * q + E], tok(gs))
                    last.then_inc(rw_ready, 1)

                def rwt_low():
                    dve.wait_ge(rwt_hi_ready, b + 1)
                    dve.tensor_tensor(rwt[32:64, :], ps7[32:64, :], rwt[32:64, :].bitcast(f32),
                                      ALU.subtract).then_inc(rwt_ready, 1)

                def p_step(n):
                    k = b * NFC + n
                    c = CHUNKS[n]
                    dve.wait_ge(v_ready, k + 1)
                    dve.wait_ge(u_moved, k + 3)
                    if n >= 2:
                        dve.wait_ge(s_ready, k - 1)
                    dve.scalar_tensor_tensor(p_sb[n % 2][:, :], v_ps(n % 2), vec[:, V_B3 + c:V_B3 + c + 1],
                                             u_sb[n % 2][:, :], ALU.add, ALU.mult).then_inc(p_ready, 1)

                def h_step(n):
                    k = b * NFC + n
                    if CHUNKS[n] >= NEC:
                        return
                    dve.wait_ge(s_ready, k + 1)
                    dve.wait_ge(rb_ready, b * NEC + (n - (NFC - NEC)) + 1)
                    dve.wait_ge(h_lo_ready, k + 1)
                    dve.tensor_tensor(h_sb[n % 3][:, :], pair(n % 2), s_sb[n % 2][:, :], ALU.mult).then_inc(h_ready, 1)

                router_a()
                router_b()
                for n in range(NFC + 1):
                    if n < NFC:
                        p_step(n)
                    if n == 2:
                        rwt_low()
                    if n >= 1:
                        h_step(n - 1)

            with dve.Fori(0, B) as b:
                batch(b)

        @block.tensor
        def _(pe):
            def three(dst, hi, lo, mhi, mlo, start=True, stop=True):
                pe.matmul(dst, hi, mhi, start=start, stop=False)
                pe.matmul(dst, hi, mlo, start=False, stop=False)
                return pe.matmul(dst, lo, mhi, start=False, stop=stop)

            pe.wait_ge(attn_in, 16 * N_ATTN_IN)
            pe.matmul(ps7[:, 0:B * Z], wkv_sb[:, 0:D], ctx_sb[:, :], start=True, stop=True).then_inc(k_proj, 1)
            pe.wait_ge(k_bias, 1)
            pe.wait_ge(wq_split, 2)

            def transposes(src, dst):
                for t in range(NT):
                    last = pe.transpose(tile_of(dst, t), tile_of(src, t), ident)
                return last

            def attention(b):
                def logits_half(half):
                    t, g = divmod(half, 2)
                    k = b * 2 * NT + half
                    if half == 0:
                        pe.wait_ge(kb_ready, 2 * b + 2)
                    pe.wait_ge(lg_sub, k + 1)
                    for q4 in range(2):
                        cols = slice(g * HALF + q4 * QUART, g * HALF + (q4 + 1) * QUART)
                        last = three(lg_ps(half % 2, q4), tile_of(q_hi, t), tile_of(q_lo, t), kb_hi[:, cols], kb_lo[:, cols])
                    last.then_inc(lg_ready, 1)

                def transpose_tile(t):
                    pe.wait_ge(exp_done, b * 2 * NT + 2 * t + 2)
                    for g in range(3):
                        k = b * 3 * NT + 3 * t + g
                        pe.wait_ge(pt_moved, k + 1)
                        for c in range(4 * g, min(4 * g + 4, NZC)):
                            last = pe.transpose(tile_of(pair((3 * t + g) % 2), c - 4 * g), tile_of(lg[t % 2], c), ident)
                        last.then_inc(pt_ps_ready, 1)

                def weigh(t):
                    pe.wait_ge(pt_moved, b * 3 * NT + 3 * t + 5)
                    if t == 0:
                        pe.wait_ge(vw_ready, 3 * b + 4)
                        pe.wait_ge(dve_pads, 1)
                    if t == 2:
                        pe.wait_ge(ao_ready, 2 * b + 1)
                    o = (t % 2) * VW_W
                    for c in range(NZC):
                        w0 = 0 if c == 0 else min(c * P // Z, HEADS - WIN_HEADS) * VC
                        w1_ = VW_W if c == 0 else w0 + WIN_HEADS * VC
                        last = pe.matmul(ps6[:, o + w0:o + w1_], tile_of(pt[t % 2], c),
                                         vw[:, c * VW_W + w0:c * VW_W + w1_], start=(c == 0), stop=(c == NZC - 1))
                    last.then_inc(av_ready, 1)

                logits_half(0)
                logits_half(1)
                for t in range(1, NT):
                    logits_half(2 * t)
                    logits_half(2 * t + 1)
                    transpose_tile(t - 1)
                    if t >= 2:
                        weigh(t - 2)
                transpose_tile(NT - 1)
                weigh(NT - 2)
                weigh(NT - 1)

            def batch(b):
                pe.wait_ge(xn_ready, 2 * b * NT + NT)
                transposes(xn, ps7).then_inc(xt_ps_ready, 1)
                pe.wait_ge(xt_hi_ready, b + 1)
                pe.wait_ge(xt_lo_ready, b + 1)
                pe.wait_ge(y_moved, b + 1)
                three(ps6[:, :], wq_hi[:, :], wq_lo[:, :], xt_hi[:, :], xt_lo[:, :]).then_inc(q_ps_ready, 1)
                pe.wait_ge(rep_ready, b + 1)
                for g in range(3):
                    dst = ps7 if g % 2 == 0 else ps6
                    if g == 1:
                        pe.wait_ge(q_hi_ready, b + 1)
                        pe.wait_ge(q_lo_ready, b + 1)
                    if g == 2:
                        pe.wait_ge(vw_ready, 3 * b + 2)
                    for c in range(4 * g, min(4 * g + 4, NZC)):
                        o = c * P % Z
                        last = pe.matmul(tile_of(dst, c - 4 * g), rep_cur[:, o:o + P], wkv_sb[:, D:2 * D], start=True, stop=True)
                    last.then_inc(vp_ready, 1)
                attention(b)
                pe.wait_ge(ao_ready, 2 * b + 2)
                transposes(ao, ps7).then_inc(aot_ps_ready, 1)
                pe.wait_ge(aot_ready, b + 1)
                for t in range(NT):
                    last = pe.matmul(tile_of(ps6, t), tile_of(aot, t), wo_sb[:, :], start=True, stop=True)
                last.then_inc(proj_ready, 1)
                pe.wait_ge(xn_ready, (2 * b + 1) * NT + NT)
                transposes(xn, ps7).then_inc(x2_ps_ready, 1)
                pe.wait_ge(x2_hi_ready, b + 1)
                pe.wait_ge(x2_lo_ready, b + 1)
                pe.wait_ge(w_split, 5)
                for t in range(NT):
                    dst = ps6[:, t * GW:(t + 1) * GW]
                    pe.matmul(dst, tile_of(x2t_hi, t), gw_hi[:, :], start=True, stop=False)
                    pe.matmul(dst, tile_of(x2t_lo, t), gw_hi[:, :], start=False, stop=False)
                    last = pe.matmul(dst, tile_of(x2t_hi, t), gw_lo[:, :], start=False, stop=True)
                last.then_inc(gate_ready, 1)

                def up(n):
                    k = b * NFC + n
                    c = CHUNKS[n]
                    pe.wait_ge(u_moved, k + 1)
                    three(u_ps(n % 2), tile_of(w1_hi, c), tile_of(w1_lo, c), x2t_hi[:, :], x2t_lo[:, :]).then_inc(u_ready, 1)
                    pe.wait_ge(p_ready, k + 1)
                    three(v_ps(n % 2), tile_of(w3_hi, c), tile_of(w3_lo, c), x2t_hi[:, :], x2t_lo[:, :]).then_inc(v_ready, 1)

                def spread(n):
                    c = CHUNKS[n]
                    e = n - (NFC - NEC)
                    if e >= 2:
                        pe.wait_ge(h_ready, b * NEC + e - 1)
                    pe.matmul(pair(n % 2), tile_of(sel, c), rwt[:, :], start=True, stop=True).then_inc(rb_ready, 1)

                def down(n):
                    k = b * NFC + n
                    c = CHUNKS[n]
                    pe.wait_ge(h_lo_ready, k + 4)
                    three(ps6[:, :], tile_of(w2_hi, c), tile_of(w2_lo, c), h_hi[n % 3][:, :], h_lo[n % 3][:, :],
                          start=(n == 0), stop=False).then_inc(down_done, 1)

                for n in range(NFC):
                    if n == 2:
                        pe.wait_ge(rw_ready, b + 1)
                        transposes(rw, ps7).then_inc(rwt_ps_ready, 1)
                    up(n)
                    if n == 2:
                        pe.wait_ge(rwt_ready, b + 1)
                    if CHUNKS[n] < NEC:
                        spread(n)
                    if n >= 3:
                        down(n - 3)
                for n in range(NFC - 3, NFC):
                    down(n)
                pe.matmul(ps6[:, :], b2_st[:, :], rwt[:, :], start=False, stop=False)
                for t in range(NT):
                    last = pe.matmul(tile_of(ps6, t), tile_of(x1, t), ident, start=False, stop=(t == NT - 1))
                last.then_inc(y_ready, 1)

            with pe.Fori(0, B) as b:
                batch(b)


def kernel(**inputs):
    import numpy as np
    import concourse.bacc as bacc
    from concourse.bass_utils import run_bass_kernel_spmd

    a = {k: np.asarray(v) for k, v in inputs.items()}
    f = np.float32

    def rows(v, n):
        flat = np.concatenate([v.reshape(-1), np.zeros(n * P - v.size, f)])
        return flat.reshape(n, P).T

    x = a["x"].reshape(B, NT, P, D).transpose(0, 2, 1, 3).reshape(B, P, NT * D)
    ctx = a["ctx_1024"].transpose(2, 0, 1)
    ctx_t = ctx.reshape(D, B * Z)
    ctx_rep = np.concatenate([ctx, ctx, ctx], axis=2).reshape(D, B * REP)

    def up(w, sw):
        return np.concatenate([w.transpose(1, 0, 2).reshape(D, E * HID), sw], axis=1)

    w2 = np.concatenate([a["L0_ffn_w2"].reshape(E * HID, D), a["L0_ffn_sw2"], np.zeros((FP - (E + 1) * HID, D), f)])
    w2 = w2.reshape(NFC, P, D).transpose(1, 0, 2).reshape(P, FP)
    b1 = np.concatenate([a["L0_ffn_b1"].reshape(-1), a["L0_ffn_sb1"]])
    b3 = np.concatenate([a["L0_ffn_b3"].reshape(-1), a["L0_ffn_sb3"]])
    vecs = np.concatenate([
        a["L0_xattn_b_q"][:, None], a["L0_xattn_b_kv"][:D, None], a["L0_xattn_b_kv"][D:, None], rows(b1, NFC), rows(b3, NFC),
        np.broadcast_to(a["L0_xattn_b_out"], (P, D)), np.broadcast_to(a["L0_ffn_gate_b"], (P, E)),
    ], axis=1)
    zrow = np.arange(HZP).reshape(NZC, P).T // Z
    consts = np.concatenate([
        np.eye(P, dtype=f),
        (np.arange(P)[:, None] // HD == np.arange(HEADS)).astype(f),
        np.where(np.arange(Z)[None, :] >= np.arange(P)[:, None], f(MASK), f(0)),
        (zrow[:, :, None] == np.arange(HEADS)).astype(f).reshape(P, NZC * HEADS),
        np.broadcast_to(np.tril(np.ones((E, E), f), -1).reshape(-1), (P, E * E)),
    ], axis=1)
    sel_rows = (np.arange(NEC * P)[None, :] // HID == np.arange(E)[:, None]).astype(f)

    arrays = {
        "x": x, "ctx_t": ctx_t, "ctx_rep": ctx_rep, "w_q": a["L0_xattn_w_q"], "w_kv": a["L0_xattn_w_kv"],
        "w_out": a["L0_xattn_w_out"], "gate_wt": a["L0_ffn_gate_w"].T,
        "w1": up(a["L0_ffn_w1"], a["L0_ffn_sw1"]), "w3": up(a["L0_ffn_w3"], a["L0_ffn_sw3"]), "w2": w2,
        "b2": np.concatenate([a["L0_ffn_b2"], a["L0_ffn_sb2"][None]]), "vecs": vecs, "consts": consts, "sel_rows": sel_rows,
    }
    arrays = {k: np.ascontiguousarray(v) for k, v in arrays.items()}
    nc = bacc.Bacc("TRN2", target_bir_lowering=False, num_devices=1)
    args = [nc.dram_tensor(k, v.shape, mybir.dt.from_np(v.dtype), kind="ExternalInput").ap() for k, v in arrays.items()]
    out = nc.dram_tensor("out", (B, D, S), mybir.dt.float32, kind="ExternalOutput").ap()
    build(nc, *args, out)
    r = run_bass_kernel_spmd(nc, [arrays], core_ids=[0])
    return r.results[0]["out"].transpose(0, 2, 1)
```

```python
from contextlib import ExitStack

import concourse.bass as bass
from concourse import mybir
from concourse.alu_op_type import AluOpType as ALU

B, S, D, Z = 4, 512, 128, 77
HEADS, HD = 16, 8
E, HID = 8, 176
P = 128
NT = S // P
HZ = HEADS * Z
NZC = -(-HZ // P)
HZP = NZC * P
HALF = HZ // 2
QUART = HZ // 4
VC = HD + 1
VW_W = HEADS * VC
WIN_HEADS = 11
NFC = -(-(E + 1) * HID // P)
NEC = E * HID // P
FP = NFC * P
BANK = 512
EPS = 1e-5
MASK = 1e12
GW = 96
REP = 3 * Z
CHUNKS = list(range(NEC, NFC)) + list(range(NEC))
assert NEC * P == E * HID

C_ID, C_HM, C_TRI, C_ZM, C_LT = 0, P, P + HEADS, P + HEADS + Z, P + HEADS + Z + NZC * HEADS
C_END = C_LT + E * E
V_BQ, V_BK, V_BV, V_B1, V_B3 = 0, 1, 2, 3, 3 + NFC
V_BO = V_B3 + NFC
V_GB = V_BO + D
V_END = V_GB + E


def build(nc, x, ctx_t, ctx_rep, w_q, w_kv, w_out, gate_wt, w1, w3, w2, b2, vecs, consts, sel_rows, out):
    f32, f32r = mybir.dt.float32, mybir.dt.float32r
    ACT = mybir.ActivationFunctionType
    AX = mybir.AxisListType.X

    st = ExitStack()
    with st:
        def sb(name, cols, dt=f32):
            return st.enter_context(nc.sbuf_tensor(name, [P, cols], dt))

        def bank(name, n=1):
            return st.enter_context(nc.psum_tensor(name, [P, n * BANK], f32))

        def sem(name):
            return st.enter_context(nc.semaphore(name))

        x_all = sb("x_all", B * S)
        xb_all = sb("xb_all", B * S)
        ctx_sb = sb("ctx_sb", B * Z)
        rep_cur = sb("rep_cur", REP)
        wq_sb = sb("wq_sb", D)
        wkv_sb = sb("wkv_sb", 2 * D)
        wo_sb = sb("wo_sb", D)
        gw_sb = sb("gw_sb", GW)
        cst = sb("cst", C_END)
        vec = sb("vec", V_END)
        w1_sb, w3_sb, w2_sb = sb("w1_sb", FP), sb("w3_sb", FP), sb("w2_sb", FP)
        b2_sb = sb("b2_sb", D)
        sel_sb = sb("sel_sb", NEC * P)
        wq_hi, wq_lo = sb("wq_hi", D, f32r), sb("wq_lo", D, f32r)
        w1_hi, w1_lo = sb("w1_hi", FP, f32r), sb("w1_lo", FP, f32r)
        w3_hi, w3_lo = sb("w3_hi", FP, f32r), sb("w3_lo", FP, f32r)
        w2_hi, w2_lo = sb("w2_hi", FP, f32r), sb("w2_lo", FP, f32r)
        b2_st = sb("b2_st", D, f32r)
        sel = sb("sel", NEC * P, f32r)
        k_f = sb("k_f", B * Z)
        k_hi, k_lo = sb("k_hi", B * Z, f32r), sb("k_lo", B * Z, f32r)
        kb_hi, kb_lo = sb("kb_hi", HZ, f32r), sb("kb_lo", HZ, f32r)
        vw = sb("vw", NZC * VW_W)
        stats1, mv1, veps1, rstd1 = sb("stats1", B * NT * 6), sb("mv1", B * NT * 2), sb("veps1", B * NT), sb("rstd1", B * NT)
        stats2, mv2, veps2, rstd2 = sb("stats2", NT * 6), sb("mv2", NT * 2), sb("veps2", NT), sb("rstd2", NT)
        nmr2 = sb("nmr2", NT)
        mhalf = sb("mhalf", B * NT)
        spare = sb("spare", 1)
        xn1, xn2 = sb("xn1", S), sb("xn2", S)
        xt_hi, xt_lo = sb("xt_hi", S, f32r), sb("xt_lo", S, f32r)
        q_hi, q_lo = sb("q_hi", S, f32r), sb("q_lo", S, f32r)
        lg = [sb(f"lg{i}", HZP) for i in range(2)]
        mx = sb("mx", 2 * HEADS)
        pt = [sb(f"pt{i}", HZP) for i in range(2)]
        rden = sb("rden", 2 * HEADS)
        ao = sb("ao", S)
        aot = sb("aot", S)
        x1 = sb("x1", S)
        x2t = sb("x2t", S)
        x2t_hi, x2t_lo = sb("x2t_hi", S, f32r), sb("x2t_lo", S, f32r)
        gmax, gsum, grec = sb("gmax", NT), sb("gsum", NT), sb("grec", NT)
        ge, gs, gbias = sb("ge", NT * E), sb("gs", NT * E), sb("gbias", NT * E)
        cgt, ceq = sb("cgt", NT * E * E), sb("ceq", NT * E * E)
        rank, chosen = sb("rank", NT * E), sb("chosen", NT * E)
        rw = sb("rw", NT * P)
        rwt = sb("rwt", S, f32r)
        u_sb = [sb(f"u_sb{i}", S) for i in range(2)]
        p_sb = [sb(f"p_sb{i}", S) for i in range(2)]
        t_sb = [sb(f"t_sb{i}", S) for i in range(2)]
        rb_sb = sb("rb_sb", S)
        pr_sb = [sb(f"pr_sb{i}", S) for i in range(2)]
        h_sb = [sb(f"h_sb{i}", S) for i in range(4)]
        h_hi = [sb(f"h_hi{i}", S, f32r) for i in range(3)]
        h_lo = [sb(f"h_lo{i}", S, f32r) for i in range(3)]
        y_sb = sb("y_sb", S)

        ps_lg = bank("ps_lg", 2)
        ps_t = bank("ps_t")
        ps_m = bank("ps_m")
        ps_u, ps_v = bank("ps_u"), bank("ps_v")
        ps_rb = bank("ps_rb")
        ps_y = bank("ps_y")

        lg_half = ps_lg[:, :].rearrange("p (a n) -> p a n", a=2)[:, :, 0:QUART].rearrange("p a (h z) -> p a h z", z=Z)
        ident = cst[:, C_ID:C_ID + P]
        bq, bk, bv = (vec[:, v:v + 1] for v in (V_BQ, V_BK, V_BV))
        vw4 = vw[:, :].rearrange("p (c h v) -> p c h v", c=NZC, h=HEADS)
        rw3 = rw[:, :].rearrange("p (t n) -> p t n", t=NT)

        def tile_of(ap, t):
            return ap[:, t * P:(t + 1) * P]

        def group(g):
            return range(4 * g, min(4 * g + 4, NZC))

        def routed(n):
            return CHUNKS[n] < NEC

        NSH = NFC - NEC

        def h_slot(n):
            return n % 3 if n else 3

        SPLIT = list(range(3, 8))
        AIDED = [2, 8, 9, 10, 11]

        def before(chunks, n):
            return sum(1 for i in chunks if i < n)

        x0_in, x_in = sem("x0_in"), sem("x_in")
        attn_in, wo_in = sem("attn_in"), sem("wo_in")
        ffn_in = sem("ffn_in")
        out_done = sem("out_done")
        pads = sem("pads")
        wq_split, k_proj, k_bias, k_split = sem("wq_split"), sem("k_proj"), sem("k_bias"), sem("k_split")
        ones_ready, xb_ready = sem("ones_ready"), sem("xb_ready")
        w2_half, w_his, w_split = sem("w2_half"), sem("w_his"), sem("w_split")
        ln1_stats, ln1_mv, ln1_eps, ln1_rstd = (sem(n) for n in ("ln1_stats", "ln1_mv", "ln1_eps", "ln1_rstd"))
        ln2_stats, ln2_mv, ln2_eps, ln2_rstd = (sem(n) for n in ("ln2_stats", "ln2_mv", "ln2_eps", "ln2_rstd"))
        ln1_done, ln2_shift = sem("ln1_done"), sem("ln2_shift")
        xn2_ready = sem("xn2_ready")
        kb_ready, rep_in, xn1_in = sem("kb_ready"), sem("rep_in"), sem("xn1_in")
        vp_ready, vw_ready = sem("vp_ready"), sem("vw_ready")
        xt_ps_ready, xt_hi_ready, xt_lo_ready = sem("xt_ps_ready"), sem("xt_hi_ready"), sem("xt_lo_ready")
        q_ps_ready, q_hi_ready, q_lo_ready = sem("q_ps_ready"), sem("q_hi_ready"), sem("q_lo_ready")
        lg_ready, lg_masked, exp_done = sem("lg_ready"), sem("lg_masked"), sem("exp_done")
        mx_ready, lg_sub = sem("mx_ready"), sem("lg_sub")
        pt_ps_ready, pt_moved = sem("pt_ps_ready"), sem("pt_moved")
        av_ready, rden_ready, ao_ready = sem("av_ready"), sem("rden_ready"), sem("ao_ready")
        aot_ps_ready, aot_ready, proj_ready, x1_ready = (sem(n) for n in ("aot_ps_ready", "aot_ready", "proj_ready", "x1_ready"))
        x2_ps_ready, x2_ready, x2_hi_ready, x2_lo_ready = (sem(n) for n in ("x2_ps_ready", "x2_ready", "x2_hi_ready", "x2_lo_ready"))
        gate_ready, gchain, gexp_ready, gsub_ready = sem("gate_ready"), sem("gchain"), sem("gexp_ready"), sem("gsub_ready")
        rw_ready, rwt_ps_ready, rwt_hi_ready, rwt_ready = (sem(n) for n in ("rw_ready", "rwt_ps_ready", "rwt_hi_ready", "rwt_ready"))
        u_ready, u_moved = sem("u_ready"), sem("u_moved")
        v_ready, p_ready = sem("v_ready"), sem("p_ready")
        t_ready, rb_ready, pr_ready, h_ready = sem("t_ready"), sem("rb_ready"), sem("pr_ready"), sem("h_ready")
        h_hi_ready = sem("h_hi_ready")
        h_lo_ready, rb_moved = sem("h_lo_ready"), sem("rb_moved")
        down_done = sem("down_done")
        y_moved = sem("y_moved")

        N_ATTN_IN, N_FFN_IN, N_PADS = 6, 10, 13


        T0 = 4

        def pipeline(engine, body):
            body(0, None)
            with engine.Fori(1, B) as a:
                body(a, a - 1)
            body(None, B - 1)

        block = st.enter_context(nc.Block())

        @block.sync
        def _(sp):
            sp.dma_start(x_all[:, 0:S], x[0, :, :]).then_inc(x0_in, 16)
            sp.dma_start(vec[:, :], vecs).then_inc(attn_in, 16)
            sp.dma_start(wkv_sb[:, :], w_kv).then_inc(attn_in, 16)
            sp.dma_start(ctx_sb[:, :], ctx_t).then_inc(attn_in, 16)
            sp.dma_start(cst[:, :], consts).then_inc(attn_in, 16)
            sp.dma_start(wq_sb[:, :], w_q).then_inc(attn_in, 16)
            sp.dma_start(rep_cur[:, :], ctx_rep[:, 0:REP]).then_inc(attn_in, 16)
            sp.dma_start(x_all[:, S:B * S].rearrange("p (b n) -> p b n", b=B - 1),
                         x[1:B, :, :].rearrange("b p n -> p b n")).then_inc(x_in, 16)
            sp.dma_start(wo_sb[:, :], w_out).then_inc(wo_in, 16)
            sp.dma_start(w1_sb[:, 0:(E + 1) * HID], w1).then_inc(ffn_in, 16)
            sp.dma_start(w3_sb[:, 0:(E + 1) * HID], w3).then_inc(ffn_in, 16)
            sp.dma_start(w2_sb[:, 0:FP - D], w2[:, 0:FP - D]).then_inc(ffn_in, 16)
            last = (E + 1) * HID - (NFC - 1) * P
            sp.wait_ge(pads, 5)
            sp.dma_start(w2_sb[0:last, FP - D:FP], w2[0:last, FP - D:FP]).then_inc(ffn_in, 16)
            sp.dma_start(gw_sb[:, 0:E], gate_wt).then_inc(ffn_in, 16)
            for q in range(3):
                sp.dma_start(b2_sb[32 * q:32 * q + E + 1, :], b2).then_inc(ffn_in, 16)
            for q in range(2):
                sp.dma_start(sel_sb[32 * q:32 * q + E, :], sel_rows).then_inc(ffn_in, 16)

            def fetch(b):
                sp.wait_ge(vp_ready, 3 * b)
                sp.dma_start(rep_cur[:, :], ctx_rep[:, bass.ds(b * REP, REP)]).then_inc(rep_in, 16)
                sp.wait_ge(ln1_done, B * NT)
                sp.wait_ge(xt_ps_ready, b)
                sp.dma_start(xn1[:, :], x_all[:, bass.ds(b * S, S)]).then_inc(xn1_in, 16)

            def store(b):
                sp.wait_ge(y_moved, b + 2)
                sp.dma_start(out[b, :, :], y_sb[:, :]).then_inc(out_done, 16)

            fetch(1)
            with sp.Fori(2, B) as b:
                fetch(b)
                store(b - 2)
            store(B - 2)
            store(B - 1)
            sp.wait_ge(out_done, 16 * (B + 1))

        @block.gpsimd
        def _(pool):
            pool.memset(mhalf[:, :], -0.5).then_inc(pads, 1)
            for pad in (w2_sb[:, FP - D:FP], b2_sb[:, :], sel_sb[:, :], gw_sb[:, :], w1_sb[:, (E + 1) * HID:FP],
                        w3_sb[:, (E + 1) * HID:FP], lg[0][:, HZ:HZP], lg[1][:, HZ:HZP], rw[:, :]):
                pool.memset(pad, 0.0).then_inc(pads, 1)
            pool.wait_ge(pads, 10)
            for q in range(3):
                pool.memset(rw3[:, :, 32 * q + E:32 * q + E + 1], 1.0).then_inc(pads, 1)

            def rstd_step(out_, in_):
                return pool.tensor_tensor(out_, in_, mhalf[:, 0:in_.shape[1]], ALU.pow)

            def keys(a):
                pool.wait_ge(mx_ready, 2 * NT * a + 1)
                for kb, k in ((kb_hi, k_hi), (kb_lo, k_lo)):
                    pool.tensor_tensor(kb[:, :].rearrange("p (h z) -> p h z", h=HEADS),
                                       k[:, bass.ds(a * Z, Z)].bitcast(f32).unsqueeze(1).broadcast_to([P, HEADS, Z]),
                                       cst[:, C_HM:C_HM + HEADS].unsqueeze(2).broadcast_to([P, HEADS, Z]),
                                       ALU.mult).then_inc(kb_ready, 1)
            def weights():
                third = slice(64, 96)
                pool.wait_ge(w_his, 1)
                pool.wait_ge(xb_ready, 1)
                pool.tensor_tensor(b2_st[third, :], b2_sb[third, :], b2_st[third, :].bitcast(f32), ALU.subtract).then_inc(w_split, 1)
                pool.wait_ge(w_split, 1)
                for i, (lo, w, hi) in enumerate(((w1_lo, w1_sb, w1_hi), (w3_lo, w3_sb, w3_hi), (w2_lo, w2_sb, w2_hi))):
                    pool.wait_ge(w_his, 2 + i)
                    pool.tensor_tensor(lo[:, :], w[:, :], hi[:, :].bitcast(f32), ALU.subtract).then_inc(w_split, 1)

            def multiply(f, n):
                pool.wait_ge(p_ready, f * NFC + n + 3)
                pool.wait_ge(rb_moved, f * len(AIDED) + before(AIDED, n) + 2)
                pool.wait_ge(h_ready, f * NFC + n - 1)
                pool.tensor_tensor(pr_sb[n % 2][:, :], rb_sb[:, :], p_sb[n % 2][:, :], ALU.mult).then_inc(pr_ready, 1)

            def lower(f, n):
                k = f * NFC + n
                pool.wait_ge(h_hi_ready, f * len(SPLIT) + before(SPLIT, n) + 1)
                pool.wait_ge(down_done, k + 1)
                pool.tensor_tensor(h_lo[n % 3][:, :], h_sb[h_slot(n)][:, :], h_hi[n % 3][:, :].bitcast(f32),
                                   ALU.subtract).then_inc(h_lo_ready, 1)

            def body(a, f):
                if f is None:
                    pool.wait_ge(ln1_eps, 1)
                    rstd_step(rstd1[:, 0:NT], veps1[:, 0:NT]).then_inc(ln1_rstd, 1)
                    pool.wait_ge(attn_in, 16 * N_ATTN_IN)
                    pool.wait_ge(k_split, 2)
                if a is not None:
                    keys(a)
                if f is None:
                    pool.wait_ge(ln1_eps, 2)
                    rstd_step(rstd1[:, NT:B * NT], veps1[:, NT:B * NT]).then_inc(ln1_rstd, 1)
                    pool.wait_ge(x_in, 16)
                    pool.wait_ge(x0_in, 16)
                    pool.tensor_tensor(xb_all[:, :].rearrange("p (t d) -> p t d", d=D),
                                       x_all[:, :].rearrange("p (t d) -> p t d", d=D),
                                       vec[:, V_BO:V_BO + D].unsqueeze(1).broadcast_to([P, B * NT, D]),
                                       ALU.add).then_inc(xb_ready, 1)
                    weights()
                for n in range(NFC):
                    if n == T0 + NT + 2 and a is not None:
                        pool.wait_ge(ln2_eps, a + 1)
                        rstd_step(rstd2[:, :], veps2[:, :]).then_inc(ln2_rstd, 1)
                    if f is not None and n in SPLIT:
                        lower(f, n)
                    if f is not None and n in AIDED:
                        multiply(f, n)

            pipeline(pool, body)

        @block.scalar
        def _(act):
            for s, credit in ((pt_moved, 1), (u_moved, 1), (y_moved, 1), (out_done, 16)):
                act.sem_inc(s, credit)
            act.wait_ge(k_proj, 1)
            act.activation(k_f[:, :], ps_t[:, 0:B * Z], ACT.Identity, bias=bk).then_inc(k_bias, 1)

            def weights(i):
                if i == 0:
                    act.wait_ge(ffn_in, 16 * N_FFN_IN)
                    act.wait_ge(pads, N_PADS)
                    act.activation(w2_sb[:, NEC * P:FP], w2_sb[:, NEC * P:FP], ACT.Copy, scale=0.5).then_inc(w2_half, 1)
                    act.activation(b2_st[:, :], b2_sb[:, :], ACT.Copy).then_inc(w_his, 1)
                if i == 2:
                    act.wait_ge(w2_half, 1)
                hi, w = ((w1_hi, w1_sb), (w3_hi, w3_sb), (w2_hi, w2_sb), (sel, sel_sb))[i]
                act.activation(hi[:, :], w[:, :], ACT.Copy).then_inc(w_his, 1)

            def normalise_2(a, tiles):
                act.wait_ge(ln2_shift, a + 1)
                for t in tiles:
                    act.activation(tile_of(xn2, t), tile_of(x1, t), ACT.Identity,
                                   bias=nmr2[:, t:t + 1], scale=rstd2[:, t:t + 1]).then_inc(xn2_ready, 1)

            def xt_upper(a):
                act.wait_ge(xt_ps_ready, a + 1)
                act.activation(xt_hi[:, :], ps_t[:, :], ACT.Copy).then_inc(xt_hi_ready, 1)

            def q_upper(a):
                act.wait_ge(q_ps_ready, a + 1)
                act.activation(q_hi[:, :], ps_m[:, :], ACT.Identity, bias=bq).then_inc(q_hi_ready, 1)

            def exps(a, half):
                t, g = divmod(half, 2)
                part = lg[t % 2][:, g * HALF:(g + 1) * HALF]
                act.wait_ge(lg_sub, a * 2 * NT + half + 2)
                act.activation(part, part, ACT.Exp).then_inc(exp_done, 1)

            def move_pt(a, t, g):
                cols = min(BANK, HZP - g * BANK)
                act.wait_ge(pt_ps_ready, a * 3 * NT + 3 * t + g + 1)
                if t >= 2 and g == 0:
                    act.wait_ge(av_ready, a * NT + t - 1)
                act.activation(pt[t % 2][:, g * BANK:g * BANK + cols], ps_t[:, 0:cols], ACT.Copy).then_inc(pt_moved, 1)

            def move_aot(a):
                act.wait_ge(aot_ps_ready, a + 1)
                act.activation(aot[:, :], ps_t[:, :], ACT.Identity, bias=bv).then_inc(aot_ready, 1)

            def move_x2(a):
                act.wait_ge(x2_ps_ready, a + 1)
                act.activation(x2t[:, :], ps_t[:, :], ACT.Copy).then_inc(x2_ready, 1)

            def x2_upper(f):
                act.wait_ge(x2_ready, f + 1)
                act.wait_ge(v_ready, f * NFC + 1)
                act.activation(x2t_hi[:, :], x2t[:, :], ACT.Copy).then_inc(x2_hi_ready, 1)

            def router_exp(f):
                act.wait_ge(gsub_ready, f + 1)
                act.activation(ge[:, :], ge[:, :], ACT.Exp).then_inc(gexp_ready, 1)

            def rwt_upper(f):
                act.wait_ge(rwt_ps_ready, f + 1)
                act.activation(rwt[:, :], ps_t[:, :], ACT.Copy).then_inc(rwt_hi_ready, 1)

            def u_step(f, n):
                k, c = f * NFC + n, CHUNKS[n]
                act.wait_ge(u_ready, k + 1)
                act.wait_ge(p_ready, k + 1)
                act.activation(u_sb[n % 2][:, :], ps_u[:, :], ACT.Identity, bias=vec[:, V_B1 + c:V_B1 + c + 1]) \
                    .then_inc(u_moved, 1)

            def move_rb(f, n):
                if n not in AIDED:
                    return
                e = f * NEC + n - NSH
                act.wait_ge(rb_ready, e + 1)
                act.wait_ge(pr_ready, e + 1)
                act.activation(rb_sb[:, :], ps_rb[:, :], ACT.Copy).then_inc(rb_moved, 1)

            def tanh_step(f, n):
                act.wait_ge(p_ready, f * NFC + n + 3)
                act.activation(t_sb[n % 2][:, :], p_sb[n % 2][:, :], ACT.Tanh, scale=0.5).then_inc(t_ready, 1)

            def upper(f, n):
                if n not in SPLIT:
                    return
                k = f * NFC + n
                act.wait_ge(h_ready, k + 1)
                act.wait_ge(down_done, k + 1)
                act.activation(h_hi[n % 3][:, :], h_sb[h_slot(n)][:, :], ACT.Copy).then_inc(h_hi_ready, 1)

            def move_y(f):
                act.wait_ge(down_done, f * NFC + NFC + 3)
                act.wait_ge(out_done, 16 * f + 16)
                act.activation(y_sb[:, :], ps_y[:, :], ACT.Copy).then_inc(y_moved, 1)

            def body(a, f):
                at, ff = a is not None, f is not None
                if at:
                    xt_upper(a)
                for n in range(1, NFC):
                    t = n - T0
                    if ff:
                        u_step(f, n)
                    if at and n == 1:
                        q_upper(a)
                    if at and 0 <= t < NT:
                        move_pt(a, t, 0)
                        move_pt(a, t, 1)
                    if ff and n == 3:
                        rwt_upper(f)
                    if ff:
                        upper(f, n - 1)
                        move_rb(f, n - 1)
                    if at and -1 <= t < NT - 1:
                        exps(a, 2 * t + 2)
                    if at and t == NT:
                        move_aot(a)
                    if at and t == NT + 3:
                        normalise_2(a, range(0, 2))
                    if ff:
                        tanh_step(f, n)
                    if at and t == NT + 3:
                        normalise_2(a, range(2, NT))
                    if at and 0 <= t < NT:
                        move_pt(a, t, 2)
                    if at and -1 <= t < NT - 1:
                        exps(a, 2 * t + 3)
                    if not ff and 0 <= t < 4:
                        weights(t)
                if at:
                    move_x2(a)
                    x2_upper(a)
                    router_exp(a)
                    u_step(a, 0)
                    tanh_step(a, 0)
                if ff:
                    move_y(f)

            pipeline(act, body)

        @block.vector
        def _(dve):
            for s, credit in ((lg_sub, 1), (mx_ready, 1), (vw_ready, 1), (p_ready, 2), (pr_ready, 1), (down_done, 3), (rb_moved, 1)):
                dve.sem_inc(s, credit)

            def ln1(first, tiles):
                for t in tiles:
                    dve.bn_stats(stats1[:, 6 * t:6 * t + 6], tile_of(x_all, t)).then_inc(ln1_stats, 1)
                for t in tiles:
                    dve.wait_ge(ln1_stats, t + 1)
                    dve.bn_aggr(mv1[:, 2 * t:2 * t + 2], stats1[:, 6 * t:6 * t + 6]).then_inc(ln1_mv, 1)
                t0, t1 = tiles[0], tiles[-1] + 1
                dve.wait_ge(ln1_mv, t1)
                dve.tensor_scalar(veps1[:, t0:t1], mv1[:, 2 * t0:2 * t1].rearrange("p (t s) -> p t s", s=2)[:, :, 1], EPS, None,
                                  ALU.add).then_inc(ln1_eps, 1)

            def normalise1(part, tiles):
                dve.wait_ge(ln1_rstd, part + 1)
                if part == 1:
                    dve.wait_ge(xb_ready, 1)
                for t in tiles:
                    dve.tensor_scalar(tile_of(xn1 if part == 0 else x_all, t), tile_of(x_all, t), mv1[:, 2 * t:2 * t + 1],
                                      rstd1[:, t:t + 1], ALU.subtract, ALU.mult).then_inc(ln1_done, 1)

            def xt_lower(a):
                dve.wait_ge(xt_hi_ready, a + 1)
                dve.tensor_tensor(xt_lo[:, :], ps_t[:, :], xt_hi[:, :].bitcast(f32), ALU.subtract).then_inc(xt_lo_ready, 1)

            def q_lower(a):
                dve.wait_ge(q_hi_ready, a + 1)
                dve.scalar_tensor_tensor(q_lo[:, :], ps_m[:, :], bq, q_hi[:, :].bitcast(f32),
                                         ALU.add, ALU.subtract).then_inc(q_lo_ready, 1)

            def values(a, g):
                c0, n = group(g)[0], len(group(g))
                dve.wait_ge(vp_ready, 3 * a + g + 1)
                dve.tensor_tensor(vw4[:, c0:c0 + n, :, 0:HD],
                                  (ps_m if g == 1 else ps_t)[:, 0:n * P].rearrange("p (c h v) -> p c h v", c=n, v=HD),
                                  cst[:, C_ZM + c0 * HEADS:C_ZM + (c0 + n) * HEADS]
                                  .rearrange("p (c h) -> p c h", c=n).unsqueeze(3).broadcast_to([P, n, HEADS, HD]),
                                  ALU.mult).then_inc(vw_ready, 1)

            def logits(a, half):
                t, g = divmod(half, 2)
                k = a * 2 * NT + half
                dst = lg[t % 2][:, g * HALF:(g + 1) * HALF].rearrange("p (a h z) -> p a h z", a=2, z=Z)
                m = mx[:, g * 8:g * 8 + 8].rearrange("p (a h) -> p a h", a=2)
                src = lg_half
                dve.wait_ge(lg_ready, k + 1)
                if half >= 4:
                    dve.wait_ge(pt_ps_ready, a * 3 * NT + 3 * (t - 1))
                if t == 0:
                    for i in range(2):
                        dve.tensor_tensor(dst[:, i], src[:, i],
                                          cst[:, C_TRI:C_TRI + Z].unsqueeze(1).broadcast_to([P, 4, Z]),
                                          ALU.subtract).then_inc(lg_masked, 1)
                    src = dst
                    dve.wait_ge(lg_masked, 4 * a + 2 * g + 2)
                dve.tensor_reduce(m, src, AX, ALU.max).then_inc(mx_ready, 1)
                dve.wait_ge(mx_ready, k + 2)
                dve.tensor_tensor(dst, src, m.unsqueeze(3).broadcast_to([P, 2, 4, Z]), ALU.subtract).then_inc(lg_sub, 1)

            def normalise(a, pr):
                src = ps_m[:, 0:2 * VW_W].rearrange("p (t h v) -> p t h v", t=2, v=VC)
                rd = rden[:, :].rearrange("p (t h) -> p t h", t=2)
                dve.wait_ge(av_ready, a * NT + 2 * pr + 2)
                dve.reciprocal(rd, src[:, :, :, HD]).then_inc(rden_ready, 1)
                dve.wait_ge(rden_ready, 2 * a + pr + 1)
                dve.tensor_tensor(ao[:, 2 * pr * P:2 * (pr + 1) * P].rearrange("p (t h v) -> p t h v", t=2, v=HD),
                                  src[:, :, :, 0:HD], rd.unsqueeze(3).broadcast_to([P, 2, HEADS, HD]),
                                  ALU.mult).then_inc(ao_ready, 1)

            def residual(a):
                dve.wait_ge(proj_ready, a + 1)
                dve.wait_ge(xb_ready, 1)
                dve.tensor_tensor(x1[:, :], ps_m[:, :], xb_all[:, bass.ds(a * S, S)], ALU.add).then_inc(x1_ready, 1)

            def stats2_step(a):
                dve.wait_ge(x1_ready, a + 1)
                for t in range(NT):
                    dve.bn_stats(stats2[:, 6 * t:6 * t + 6], tile_of(x1, t)).then_inc(ln2_stats, 1)

            def ln2(a):
                dve.wait_ge(ln2_stats, a * NT + NT)
                dve.memset(spare[:, :], 0.0)
                for t in range(NT):
                    dve.bn_aggr(mv2[:, 2 * t:2 * t + 2], stats2[:, 6 * t:6 * t + 6]).then_inc(ln2_mv, 1)
                dve.wait_ge(ln2_mv, a * NT + NT)
                dve.tensor_scalar(veps2[:, :], mv2[:, :].rearrange("p (t s) -> p t s", s=2)[:, :, 1], EPS, None,
                                  ALU.add).then_inc(ln2_eps, 1)

            def shift2(a):
                dve.wait_ge(ln2_rstd, a + 1)
                dve.scalar_tensor_tensor(nmr2[:, :], mv2[:, :].rearrange("p (t s) -> p t s", s=2)[:, :, 0], -1.0,
                                         rstd2[:, :], ALU.mult, ALU.mult).then_inc(ln2_shift, 1)

            def x2_lower(f):
                dve.wait_ge(x2_hi_ready, f + 1)
                dve.tensor_tensor(x2t_lo[:, :], x2t[:, :], x2t_hi[:, :].bitcast(f32), ALU.subtract).then_inc(x2_lo_ready, 1)

            LINKS = 11

            def link(f, i, ins):
                ins.then_inc(gchain, 1)
                dve.wait_ge(gchain, f * LINKS + i)

            def per_token(ap):
                return ap[:, :].unsqueeze(2).broadcast_to([P, NT, E])

            def tok(ap):
                return ap[:, :].rearrange("p (t e) -> p t e", t=NT)

            def router_scores(f):
                scores = ps_m[:, 0:NT * GW].rearrange("p (t n) -> p t n", t=NT)[:, :, 0:E]
                dve.wait_ge(gate_ready, f + 1)
                link(f, 1, dve.tensor_reduce(gmax[:, :], scores, AX, ALU.max))
                dve.tensor_tensor(tok(ge), scores, per_token(gmax), ALU.subtract).then_inc(gsub_ready, 1)

            def router_softmax(f):
                dve.wait_ge(gexp_ready, f + 1)
                link(f, 2, dve.tensor_reduce(gsum[:, :], tok(ge), AX, ALU.add))
                link(f, 3, dve.reciprocal(grec[:, :], gsum[:, :]))
                link(f, 4, dve.tensor_tensor(tok(gs), tok(ge), per_token(grec), ALU.mult))
                link(f, 5, dve.tensor_tensor(tok(gbias), tok(gs),
                                             vec[:, V_GB:V_GB + E].unsqueeze(1).broadcast_to([P, NT, E]), ALU.add))

            def router_compare(f):
                mine = tok(gbias).unsqueeze(3).broadcast_to([P, NT, E, E])
                others = tok(gbias).unsqueeze(2).broadcast_to([P, NT, E, E])
                dve.tensor_tensor(cgt[:, :].rearrange("p (t e f) -> p t e f", e=E, f=E), others, mine, ALU.is_gt)
                last = dve.tensor_tensor(ceq[:, :].rearrange("p (t e f) -> p t e f", e=E, f=E), others, mine, ALU.is_equal)
                last.then_inc(gchain, 1)

            def router_choose(f):
                dve.wait_ge(gchain, f * LINKS + 6)
                eqt = ceq[:, :].rearrange("p (t n) -> p t n", t=NT)
                link(f, 7, dve.tensor_tensor(eqt, eqt, cst[:, C_LT:C_LT + E * E].unsqueeze(1).broadcast_to([P, NT, E * E]), ALU.mult))
                link(f, 8, dve.tensor_tensor(cgt[:, :], cgt[:, :], ceq[:, :], ALU.add))
                link(f, 9, dve.tensor_reduce(rank[:, :], cgt[:, :].rearrange("p (n f) -> p n f", f=E), AX, ALU.add))
                link(f, 10, dve.tensor_scalar(chosen[:, :], rank[:, :], 2.0, None, ALU.is_lt))
                link(f, 11, dve.tensor_tensor(tok(gs), tok(gs), tok(chosen), ALU.mult))
                for q in range(3):
                    last = dve.tensor_copy(rw3[:, :, 32 * q:32 * q + E], tok(gs))
                last.then_inc(rw_ready, 1)

            def rwt_lower(f):
                dve.wait_ge(rwt_hi_ready, f + 1)
                dve.tensor_tensor(rwt[32:64, :], ps_t[32:64, :], rwt[32:64, :].bitcast(f32),
                                  ALU.subtract).then_inc(rwt_ready, 1)

            def p_step(f, n):
                k, c = f * NFC + n, CHUNKS[n]
                dve.wait_ge(v_ready, k + 2)
                dve.wait_ge(u_moved, k + 2)
                if n >= 2:
                    dve.wait_ge(t_ready, k - 1)
                    if not routed(n - 2):
                        dve.wait_ge(h_ready, k - 1)
                dve.scalar_tensor_tensor(p_sb[n % 2][:, :], ps_v[:, :], vec[:, V_B3 + c:V_B3 + c + 1],
                                         u_sb[n % 2][:, :], ALU.add, ALU.mult).then_inc(p_ready, 1)

            def multiply(f, n):
                if routed(n) and n not in AIDED:
                    k, e = f * NFC + n, f * NEC + n - NSH
                    dve.wait_ge(h_ready, k - 1)
                    dve.wait_ge(p_ready, k + 3)
                    dve.wait_ge(rb_ready, e + 1)
                    dve.tensor_tensor(pr_sb[n % 2][:, :], ps_rb[:, :], p_sb[n % 2][:, :], ALU.mult).then_inc(pr_ready, 1)

            def gate(f, n):
                k, src = f * NFC + n, p_sb[n % 2]
                if routed(n):
                    dve.wait_ge(pr_ready, f * NEC + n - NSH + 2)
                    src = pr_sb[n % 2]
                dve.wait_ge(t_ready, k + 1)
                dve.wait_ge(down_done, k + 1)
                dve.scalar_tensor_tensor(h_sb[h_slot(n)][:, :], t_sb[n % 2][:, :], 1.0, src[:, :],
                                         ALU.add, ALU.mult).then_inc(h_ready, 1)

            def body(a, f):
                at, ff = a is not None, f is not None
                if not ff:
                    dve.wait_ge(x0_in, 16)
                    ln1(0, range(0, NT))
                    dve.wait_ge(attn_in, 16 * N_ATTN_IN)
                    dve.tensor_copy(wq_hi[:, :], wq_sb[:, :]).then_inc(wq_split, 1)
                    dve.wait_ge(wq_split, 1)
                    dve.tensor_tensor(wq_lo[:, :], wq_sb[:, :], wq_hi[:, :].bitcast(f32), ALU.subtract).then_inc(wq_split, 1)
                    dve.wait_ge(k_bias, 1)
                    dve.tensor_copy(k_hi[:, :], k_f[:, :]).then_inc(k_split, 1)
                    dve.wait_ge(k_split, 1)
                    dve.tensor_tensor(k_lo[:, :], k_f[:, :], k_hi[:, :].bitcast(f32), ALU.subtract).then_inc(k_split, 1)
                    dve.wait_ge(pads, N_PADS)
                    normalise1(0, range(0, NT))
                    dve.tensor_copy(vw4[:, :, :, HD], cst[:, C_ZM:C_ZM + NZC * HEADS].rearrange("p (c h) -> p c h", c=NZC)) \
                        .then_inc(ones_ready, 1)
                if ff:
                    router_softmax(f)
                    gate(f, 0)
                if at:
                    xt_lower(a)
                for n in range(1, NFC):
                    t = n - T0
                    if at and t == 2:
                        normalise(a, 0)
                    if at and t == NT:
                        normalise(a, 1)
                    if at and t == NT + 1:
                        residual(a)
                    if at and t == NT + 2:
                        ln2(a)
                    if ff and n >= 4:
                        multiply(f, n - 1)
                        if n - 1 in SPLIT:
                            gate(f, n - 1)
                    if at and 0 <= t < NT - 1:
                        logits(a, 2 * t + 2)
                    if ff and n == 1:
                        p_step(f, n)
                        router_compare(f)
                    if at and n == 1:
                        q_lower(a)
                    if ff and n == 1:
                        router_choose(f)
                    if at and n == 2:
                        values(a, 0)
                    if ff and n == 2:
                        p_step(f, n)
                    if at and n == 2:
                        values(a, 1)
                    if ff and n == 2:
                        gate(f, 1)
                    if ff and n == 3:
                        rwt_lower(f)
                    if ff and n >= 3:
                        p_step(f, n)
                    if at and n == 3:
                        logits(a, 0)
                        values(a, 2)
                        logits(a, 1)
                    if ff and n >= 3 and n - 1 not in SPLIT:
                        gate(f, n - 1)
                    if at and 0 <= t < NT - 1:
                        logits(a, 2 * t + 3)
                    if at and t == NT + 1:
                        stats2_step(a)
                    if at and t == NT + 2:
                        shift2(a)
                    if not ff and n == 1:
                        dve.wait_ge(x_in, 16)
                        ln1(1, range(NT, B * NT))
                    if not ff and n == 4:
                        normalise1(1, range(NT, B * NT))
                if ff:
                    multiply(f, NFC - 1)
                if at:
                    x2_lower(a)
                if ff:
                    gate(f, NFC - 1)
                if at:
                    router_scores(a)
                    p_step(a, 0)

            pipeline(dve, body)

        @block.tensor
        def _(pe):
            pe.sem_inc(v_ready, 1)

            def three(dst, hi, lo, mhi, mlo, start=True, stop=True):
                pe.matmul(dst, hi, mhi, start=start, stop=False)
                pe.matmul(dst, hi, mlo, start=False, stop=False)
                return pe.matmul(dst, lo, mhi, start=False, stop=stop)

            def transposes(src):
                for t in range(NT):
                    last = pe.transpose(tile_of(ps_t, t), tile_of(src, t), ident)
                return last

            pe.wait_ge(attn_in, 16 * N_ATTN_IN)
            pe.matmul(ps_t[:, 0:B * Z], wkv_sb[:, 0:D], ctx_sb[:, :], start=True, stop=True).then_inc(k_proj, 1)
            pe.wait_ge(k_bias, 1)

            def turn_x(a):
                if type(a) is int:
                    pe.wait_ge(ln1_done, NT)
                else:
                    pe.wait_ge(xn1_in, 16 * a)
                transposes(xn1).then_inc(xt_ps_ready, 1)

            def queries(a, f):
                pe.wait_ge(xt_hi_ready, a + 1)
                pe.wait_ge(xt_lo_ready, a + 1)
                if f is None:
                    pe.wait_ge(wq_split, 2)
                else:
                    pe.wait_ge(gsub_ready, f + 1)
                three(ps_m[:, :], wq_hi[:, :], wq_lo[:, :], xt_hi[:, :], xt_lo[:, :]).then_inc(q_ps_ready, 1)

            def values(a, g, f):
                if g == 0:
                    if type(a) is not int:
                        pe.wait_ge(rep_in, 16 * a)
                    pe.wait_ge(xt_hi_ready, a + 1)
                    pe.wait_ge(xt_lo_ready, a + 1)
                elif g == 1:
                    pe.wait_ge(q_hi_ready, a + 1)
                    pe.wait_ge(q_lo_ready, a + 1)
                elif f is not None:
                    pe.wait_ge(rwt_ready, f + 1)
                else:
                    pe.wait_ge(vw_ready, 3 * a + 2)
                dst = ps_m if g == 1 else ps_t
                for c in group(g):
                    o = c * P % Z
                    last = pe.matmul(tile_of(dst, c - 4 * g), rep_cur[:, o:o + P], wkv_sb[:, D:2 * D], start=True, stop=True)
                last.then_inc(vp_ready, 1)

            def logits(a, half):
                t, g = divmod(half, 2)
                k = a * 2 * NT + half
                if half == 0:
                    pe.wait_ge(kb_ready, 2 * a + 2)
                    pe.wait_ge(q_hi_ready, a + 1)
                    pe.wait_ge(q_lo_ready, a + 1)
                pe.wait_ge(lg_sub, k + 1)
                for i in range(2):
                    cols = slice(g * HALF + i * QUART, g * HALF + (i + 1) * QUART)
                    last = three(ps_lg[:, i * BANK:i * BANK + QUART], tile_of(q_hi, t), tile_of(q_lo, t), kb_hi[:, cols], kb_lo[:, cols])
                last.then_inc(lg_ready, 1)

            def turn_probs(a, t, g):
                k = a * 3 * NT + 3 * t + g
                if g == 0:
                    pe.wait_ge(exp_done, a * 2 * NT + 2 * t + 2)
                    if t == 0:
                        pe.wait_ge(vw_ready, 3 * a + 4)
                pe.wait_ge(pt_moved, k + 1)
                for c in group(g):
                    last = pe.transpose(tile_of(ps_t, c - 4 * g), tile_of(lg[t % 2], c), ident)
                last.then_inc(pt_ps_ready, 1)

            def weigh(a, t):
                pe.wait_ge(pt_moved, a * 3 * NT + 3 * t + 4)
                if t == 0:
                    pe.wait_ge(vw_ready, 3 * a + 4)
                    pe.wait_ge(ones_ready, 1)
                if t == 2:
                    pe.wait_ge(ao_ready, 2 * a + 1)
                o = (t % 2) * VW_W
                for c in range(NZC):
                    w0 = 0 if c == 0 else min(c * P // Z, HEADS - WIN_HEADS) * VC
                    w1_ = VW_W if c == 0 else w0 + WIN_HEADS * VC
                    last = pe.matmul(ps_m[:, o + w0:o + w1_], tile_of(pt[t % 2], c),
                                     vw[:, c * VW_W + w0:c * VW_W + w1_], start=(c == 0), stop=(c == NZC - 1))
                last.then_inc(av_ready, 1)

            def turn_ao(a):
                pe.wait_ge(ao_ready, 2 * a + 2)
                transposes(ao).then_inc(aot_ps_ready, 1)

            def project(a):
                pe.wait_ge(aot_ready, a + 1)
                pe.wait_ge(wo_in, 16)
                for t in range(NT):
                    last = pe.matmul(tile_of(ps_m, t), tile_of(aot, t), wo_sb[:, :], start=True, stop=True)
                last.then_inc(proj_ready, 1)

            def turn_x2(a):
                pe.wait_ge(xn2_ready, a * NT + NT)
                transposes(xn2).then_inc(x2_ps_ready, 1)

            def router(a):
                pe.wait_ge(x2_ready, a + 1)
                pe.wait_ge(ffn_in, 16 * N_FFN_IN)
                for t in range(NT):
                    last = pe.matmul(ps_m[:, t * GW:(t + 1) * GW], tile_of(x2t, t), gw_sb[:, :], start=True, stop=True)
                last.then_inc(gate_ready, 1)

            def up_u(f, n):
                k, c = f * NFC + n, CHUNKS[n]
                pe.wait_ge(u_moved, k + 1)
                three(ps_u[:, :], tile_of(w1_hi, c), tile_of(w1_lo, c), x2t_hi[:, :], x2t_lo[:, :]).then_inc(u_ready, 1)

            def up_v(f, n):
                k, c = f * NFC + n, CHUNKS[n]
                pe.wait_ge(p_ready, k + 2)
                three(ps_v[:, :], tile_of(w3_hi, c), tile_of(w3_lo, c), x2t_hi[:, :], x2t_lo[:, :]).then_inc(v_ready, 1)

            def spread(f, n):
                if n - 1 in AIDED:
                    pe.wait_ge(rb_moved, f * len(AIDED) + before(AIDED, n - 1) + 2)
                else:
                    pe.wait_ge(pr_ready, f * NEC + n - NSH + 1)
                pe.matmul(ps_rb[:, :], tile_of(sel, CHUNKS[n]), rwt[:, :], start=True, stop=True).then_inc(rb_ready, 1)

            def down(f, n, stop=False):
                c = CHUNKS[n]
                if n in SPLIT:
                    pe.wait_ge(h_lo_ready, f * len(SPLIT) + before(SPLIT, n) + 1)
                else:
                    pe.wait_ge(h_ready, f * NFC + n + 1)
                    return pe.matmul(ps_y[:, :], tile_of(w2_sb, c), h_sb[h_slot(n)][:, :], start=False, stop=stop).then_inc(down_done, 1)
                return three(ps_y[:, :], tile_of(w2_hi, c), tile_of(w2_lo, c), h_hi[n % 3][:, :], h_lo[n % 3][:, :],
                             start=False, stop=stop).then_inc(down_done, 1)

            def start_y(f):
                pe.wait_ge(rwt_ready, f + 1)
                pe.wait_ge(y_moved, f + 1)
                pe.matmul(ps_y[:, :], b2_st[:, :], rwt[:, :], start=True, stop=False)
                for t in range(NT):
                    pe.matmul(tile_of(ps_y, t), tile_of(x1, t), ident, start=False, stop=False)

            def turn_rw(a, f):
                pe.wait_ge(rw_ready, f + 1)
                if a is not None:
                    pe.wait_ge(vw_ready, 3 * a + 2)
                transposes(rw).then_inc(rwt_ps_ready, 1)

            def body(a, f):
                at, ff = a is not None, f is not None
                if at:
                    turn_x(a)
                for n in range(1, NFC):
                    t = n - T0
                    if ff:
                        up_u(f, n)
                    if ff and n == 1:
                        up_v(f, n)
                    if at and n == 1:
                        queries(a, f)
                        values(a, 0, f)
                    if at and n == 2:
                        values(a, 1, f)
                    if ff and n == 2:
                        up_v(f, n)
                    if at and n == 3:
                        logits(a, 0)
                    if ff and n == 3:
                        turn_rw(a, f)
                        up_v(f, n)
                        start_y(f)
                    if ff and n >= 3:
                        spread(f, n - 1)
                    if ff and n in (3, 4):
                        down(f, n - 3)
                    if ff and n == 4:
                        up_v(f, n)
                    if at and n == 3:
                        values(a, 2, f)
                        logits(a, 1)
                    if at and 0 <= t < NT:
                        turn_probs(a, t, 0)
                    if at and 0 <= t < NT - 1:
                        logits(a, 2 * t + 2)
                    if ff and t == NT - 1:
                        down(f, n - 3)
                    if at and 0 <= t < NT:
                        turn_probs(a, t, 1)
                    if ff and n > 4 and t != NT - 1:
                        down(f, n - 3)
                    if at and t == NT + 1:
                        project(a)
                    if at and n == NFC - 1:
                        turn_x2(a)
                    if ff and n > 4:
                        up_v(f, n)
                    if at and 0 <= t < NT:
                        turn_probs(a, t, 2)
                    if at and 0 <= t < NT - 1:
                        logits(a, 2 * t + 3)
                    if at and 0 <= t < NT:
                        weigh(a, t)
                    if at and t == NT:
                        turn_ao(a)
                if ff:
                    spread(f, NFC - 1)
                    down(f, NFC - 3)
                if at:
                    router(a)
                    pe.wait_ge(w_split, 4)
                    pe.wait_ge(x2_hi_ready, a + 1)
                    pe.wait_ge(x2_lo_ready, a + 1)
                    up_u(a, 0)
                    up_v(a, 0)
                if ff:
                    down(f, NFC - 2)
                    down(f, NFC - 1, stop=True)

            pipeline(pe, body)


def kernel(**inputs):
    import numpy as np
    import concourse.bacc as bacc
    from concourse.bass_utils import run_bass_kernel_spmd

    a = {k: np.asarray(v) for k, v in inputs.items()}
    f = np.float32

    def rows(v, n):
        flat = np.concatenate([v.reshape(-1), np.zeros(n * P - v.size, f)])
        return flat.reshape(n, P).T

    x = a["x"].reshape(B, NT, P, D).transpose(0, 2, 1, 3).reshape(B, P, NT * D)
    ctx = a["ctx_1024"].transpose(2, 0, 1)
    ctx_t = ctx.reshape(D, B * Z)
    ctx_rep = np.concatenate([ctx, ctx, ctx], axis=2).reshape(D, B * REP)

    def up(w, sw):
        return np.concatenate([w.transpose(1, 0, 2).reshape(D, E * HID), sw], axis=1)

    w2 = np.concatenate([a["L0_ffn_w2"].reshape(E * HID, D), a["L0_ffn_sw2"], np.zeros((FP - (E + 1) * HID, D), f)])
    w2 = w2.reshape(NFC, P, D).transpose(1, 0, 2).reshape(P, FP)
    b1 = np.concatenate([a["L0_ffn_b1"].reshape(-1), a["L0_ffn_sb1"]])
    b3 = np.concatenate([a["L0_ffn_b3"].reshape(-1), a["L0_ffn_sb3"]])
    vecs = np.concatenate([
        a["L0_xattn_b_q"][:, None], a["L0_xattn_b_kv"][:D, None], a["L0_xattn_b_kv"][D:, None], rows(b1, NFC), rows(b3, NFC),
        np.broadcast_to(a["L0_xattn_b_out"], (P, D)), np.broadcast_to(a["L0_ffn_gate_b"], (P, E)),
    ], axis=1)
    zrow = np.arange(HZP).reshape(NZC, P).T // Z
    consts = np.concatenate([
        np.eye(P, dtype=f),
        (np.arange(P)[:, None] // HD == np.arange(HEADS)).astype(f),
        np.where(np.arange(Z)[None, :] >= np.arange(P)[:, None], f(MASK), f(0)),
        (zrow[:, :, None] == np.arange(HEADS)).astype(f).reshape(P, NZC * HEADS),
        np.broadcast_to(np.tril(np.ones((E, E), f), -1).reshape(-1), (P, E * E)),
    ], axis=1)
    sel_rows = np.where(np.arange(NEC * P)[None, :] // HID == np.arange(E)[:, None], f(0.5), f(0))

    arrays = {
        "x": x, "ctx_t": ctx_t, "ctx_rep": ctx_rep, "w_q": a["L0_xattn_w_q"], "w_kv": a["L0_xattn_w_kv"],
        "w_out": a["L0_xattn_w_out"], "gate_wt": a["L0_ffn_gate_w"].T,
        "w1": up(a["L0_ffn_w1"], a["L0_ffn_sw1"]), "w3": up(a["L0_ffn_w3"], a["L0_ffn_sw3"]), "w2": w2,
        "b2": np.concatenate([a["L0_ffn_b2"], a["L0_ffn_sb2"][None]]), "vecs": vecs, "consts": consts, "sel_rows": sel_rows,
    }
    arrays = {k: np.ascontiguousarray(v) for k, v in arrays.items()}
    nc = bacc.Bacc("TRN2", target_bir_lowering=False, num_devices=1)
    args = [nc.dram_tensor(k, v.shape, mybir.dt.from_np(v.dtype), kind="ExternalInput").ap() for k, v in arrays.items()]
    out = nc.dram_tensor("out", (B, D, S), mybir.dt.float32, kind="ExternalOutput").ap()
    build(nc, *args, out)
    r = run_bass_kernel_spmd(nc, [arrays], core_ids=[0])
    return r.results[0]["out"].transpose(0, 2, 1)
```

```python
from contextlib import ExitStack

import concourse.bass as bass
from concourse import mybir
from concourse.alu_op_type import AluOpType as ALU

B, S, D, Z = 4, 512, 128, 77
HEADS, HD = 16, 8
E, HID = 8, 176
P = 128
NT = S // P
HZ = HEADS * Z
NZC = -(-HZ // P)
HZP = NZC * P
HALF = HZ // 2
QUART = HZ // 4
VC = HD + 1
VW_W = HEADS * VC
WIN_HEADS = 11
NFC = -(-(E + 1) * HID // P)
NEC = E * HID // P
FP = NFC * P
BANK = 512
EPS = 1e-5
MASK = 1e12
GW = 96
CHUNKS = list(range(NEC, NFC)) + list(range(NEC))
assert NEC * P == E * HID
PIECES = [(c, h, max(c * P, h * Z), min((c + 1) * P, (h + 1) * Z)) for h in range(HEADS)
          for c in range(h * Z // P, ((h + 1) * Z - 1) // P + 1)]

C_ID, C_HM, C_TRI, C_ZM, C_LT = 0, P, P + HEADS, P + HEADS + Z, P + HEADS + Z + NZC * HEADS
C_END = C_LT + E * E
V_BQ, V_BK, V_BV, V_B1, V_B3 = 0, 1, 2, 3, 3 + NFC
V_BO = V_B3 + NFC
V_GB = V_BO + D
V_END = V_GB + E


def build(nc, x, ctx_t, w_q, w_kv, w_out, gate_wt, w1, w3, w2, b2, vecs, consts, sel_rows, out):
    f32, f32r = mybir.dt.float32, mybir.dt.float32r
    ACT = mybir.ActivationFunctionType
    AX = mybir.AxisListType.X

    st = ExitStack()
    with st:
        def sb(name, cols, dt=f32):
            return st.enter_context(nc.sbuf_tensor(name, [P, cols], dt))

        def bank(name, n=1):
            return st.enter_context(nc.psum_tensor(name, [P, n * BANK], f32))

        def sem(name):
            return st.enter_context(nc.semaphore(name))

        x_all = sb("x_all", B * S)
        xb_all = sb("xb_all", B * S)
        ctx_sb = sb("ctx_sb", B * Z)
        wq_sb = sb("wq_sb", D)
        wkv_sb = sb("wkv_sb", 2 * D)
        wo_sb = sb("wo_sb", D)
        gw_sb = sb("gw_sb", GW)
        cst = sb("cst", C_END)
        vec = sb("vec", V_END)
        w2_sb = sb("w2_sb", FP)
        b2_sb = sb("b2_sb", D)
        sel_sb = sb("sel_sb", NEC * P)
        w1_hi, w1_lo = sb("w1_hi", FP, f32r), sb("w1_lo", FP, f32r)
        w3_hi, w3_lo = sb("w3_hi", FP, f32r), sb("w3_lo", FP, f32r)
        w2_hi, w2_lo = sb("w2_hi", FP, f32r), sb("w2_lo", FP, f32r)
        b2_st = sb("b2_st", D, f32r)
        sel = sb("sel", NEC * P, f32r)
        k_f = sb("k_f", B * Z)
        k_hi, k_lo = sb("k_hi", B * Z, f32r), sb("k_lo", B * Z, f32r)
        kb_hi, kb_lo = sb("kb_hi", HZ, f32r), sb("kb_lo", HZ, f32r)
        v_sb = sb("v_sb", B * D)
        vw = sb("vw", B * NZC * VW_W)
        stats1, mv1, veps1, rstd1 = sb("stats1", B * NT * 6), sb("mv1", B * NT * 2), sb("veps1", B * NT), sb("rstd1", B * NT)
        stats2, mv2, veps2, rstd2 = sb("stats2", NT * 6), sb("mv2", NT * 2), sb("veps2", NT), sb("rstd2", NT)
        nmr2 = sb("nmr2", NT)
        mhalf = sb("mhalf", B * NT)
        spare = sb("spare", 1)
        xn1, xn2 = sb("xn1", S), sb("xn2", S)
        xt = sb("xt", S)
        q_hi, q_lo = sb("q_hi", S, f32r), sb("q_lo", S, f32r)
        lg = [sb(f"lg{i}", HZP) for i in range(2)]
        mx = sb("mx", 2 * HEADS)
        pt = [sb(f"pt{i}", HZP) for i in range(2)]
        rden = sb("rden", 2 * HEADS)
        ao = sb("ao", S)
        aot = sb("aot", S)
        x1 = sb("x1", S)
        x2t = sb("x2t", S)
        x2t_hi, x2t_lo = sb("x2t_hi", S, f32r), sb("x2t_lo", S, f32r)
        gmax, gsum, grec = sb("gmax", NT), sb("gsum", NT), sb("grec", NT)
        ge, gs, gbias = sb("ge", NT * E), sb("gs", NT * E), sb("gbias", NT * E)
        cgt, ceq = sb("cgt", NT * E * E), sb("ceq", NT * E * E)
        rank, chosen = sb("rank", NT * E), sb("chosen", NT * E)
        rw_hi = sb("rw_hi", NT * E, f32r)
        rw = sb("rw", NT * P)
        rwt = sb("rwt", S, f32r)
        up_work, tr_work = sb("up_work", 4 * S), sb("tr_work", 4 * S)
        u_sb, p_sb = ([up_work[:, (i + j) * S:(i + j + 1) * S] for j in range(2)] for i in (0, 2))
        t_sb, pr_sb = ([tr_work[:, (i + j) * S:(i + j + 1) * S] for j in range(2)] for i in (0, 2))
        w1_sb, w3_sb = up_work[:, 0:FP], tr_work[:, 0:FP]
        rb_sb = sb("rb_sb", S)
        h_sb = [sb(f"h_sb{i}", S) for i in range(4)]
        h_hi = [sb(f"h_hi{i}", S, f32r) for i in range(3)]
        h_lo = [sb(f"h_lo{i}", S, f32r) for i in range(3)]
        y_sb = sb("y_sb", S)

        ps_lg = bank("ps_lg", 2)
        ps_t = bank("ps_t")
        ps_m = bank("ps_m")
        ps_u, ps_v = bank("ps_u"), bank("ps_v")
        ps_rby = bank("ps_rby", 2)
        ps_rb = ps_rby[:, 0:BANK]
        ps_y = ps_rby[:, BANK:2 * BANK]

        ident = cst[:, C_ID:C_ID + P]
        bq, bk, bv = (vec[:, v:v + 1] for v in (V_BQ, V_BK, V_BV))
        vw4 = vw[:, :].rearrange("p (b c n) -> p b c n", b=B, c=NZC)
        rw3 = rw[:, :].rearrange("p (t n) -> p t n", t=NT)

        def tile_of(ap, t):
            return ap[:, t * P:(t + 1) * P]

        def turn_bank(f, g):
            return ps_t if f is not None else (ps_t, ps_u, ps_v)[g]

        def lg_banks(f, half):
            return ps_rby if f is None and half % 2 else ps_lg

        def group(g):
            return range(4 * g, min(4 * g + 4, NZC))

        def routed(n):
            return CHUNKS[n] < NEC

        NSH = NFC - NEC

        def h_slot(n):
            return n % 3 if n else 3

        SPLIT = list(range(3, 8))
        AIDED = [2, 8, 9, 10, 11]
        ALONE = [n for n in range(NFC) if routed(n) and n not in AIDED]

        def before(chunks, n):
            return sum(1 for i in chunks if i < n)

        x0_in, x_in = sem("x0_in"), sem("x_in")
        kv_in = sem("kv_in")
        attn_in, wo_in = sem("attn_in"), sem("wo_in")
        ffn_in = sem("ffn_in")
        out_done = sem("out_done")
        pads = sem("pads")
        k_proj, k_bias, k_split = sem("k_proj"), sem("k_bias"), sem("k_split")
        ones_ready, xb_ready = sem("ones_ready"), sem("xb_ready")
        w2_half, w_his, w_split, w2_split = (sem(n) for n in ("w2_half", "w_his", "w_split", "w2_split"))
        ln1_stats, ln1_mv, ln1_eps, ln1_rstd = (sem(n) for n in ("ln1_stats", "ln1_mv", "ln1_eps", "ln1_rstd"))
        ln2_stats, ln2_mv, ln2_eps, ln2_rstd = (sem(n) for n in ("ln2_stats", "ln2_mv", "ln2_eps", "ln2_rstd"))
        ln1_done, ln2_shift = sem("ln1_done"), sem("ln2_shift")
        xn2_ready = sem("xn2_ready")
        kb_ready, kb_lo_ready, xn1_in = sem("kb_ready"), sem("kb_lo_ready"), sem("xn1_in")
        vp_ready, v_moved, vw_zero, vw_zero_rest = (sem(n) for n in ("vp_ready", "v_moved", "vw_zero", "vw_zero_rest"))
        vw_in, vw_rest_in = sem("vw_in"), sem("vw_rest_in")
        xt_ps_ready, xt_ready = sem("xt_ps_ready"), sem("xt_ready")
        q_ps_ready, q_hi_ready, q_lo_ready = sem("q_ps_ready"), sem("q_hi_ready"), sem("q_lo_ready")
        lg_ready, lg_masked, exp_done = sem("lg_ready"), sem("lg_masked"), sem("exp_done")
        mx_ready, lg_sub = sem("mx_ready"), sem("lg_sub")
        pt_ps_ready, pt_moved = sem("pt_ps_ready"), sem("pt_moved")
        av_ready, rden_ready, ao_ready = sem("av_ready"), sem("rden_ready"), sem("ao_ready")
        aot_ps_ready, aot_ready, proj_ready, x1_ready = (sem(n) for n in ("aot_ps_ready", "aot_ready", "proj_ready", "x1_ready"))
        x2_ps_ready, x2_ready, x2_hi_ready, x2_lo_ready = (sem(n) for n in ("x2_ps_ready", "x2_ready", "x2_hi_ready", "x2_lo_ready"))
        gate_ready, gchain, gexp_ready, gsub_ready = sem("gate_ready"), sem("gchain"), sem("gexp_ready"), sem("gsub_ready")
        rw_ready, rwt_ps_ready, rwt_ready = (sem(n) for n in ("rw_ready", "rwt_ps_ready", "rwt_ready"))
        u_ready, u_moved = sem("u_ready"), sem("u_moved")
        v_ready, p_ready = sem("v_ready"), sem("p_ready")
        t_ready, rb_ready, pr_ready, h_ready = sem("t_ready"), sem("rb_ready"), sem("pr_ready"), sem("h_ready")
        h_hi_ready = sem("h_hi_ready")
        h_lo_ready, rb_moved, pr_aided = sem("h_lo_ready"), sem("rb_moved"), sem("pr_aided")
        down_done = sem("down_done")
        y_moved = sem("y_moved")

        N_KV_IN, N_ATTN_IN, N_FFN_IN, N_PADS = 3, 2, 10, 12


        def pipeline(engine, first, both, last):
            first()
            with engine.Fori(1, B) as a:
                both(a, a - 1)
            last(B - 1)

        def spread_keys(engine, kb, k, a):
            return engine.tensor_tensor(kb[:, :].rearrange("p (h z) -> p h z", h=HEADS),
                                        k[:, bass.ds(a * Z, Z)].bitcast(f32).unsqueeze(1).broadcast_to([P, HEADS, Z]),
                                        cst[:, C_HM:C_HM + HEADS].unsqueeze(2).broadcast_to([P, HEADS, Z]), ALU.mult)

        block = st.enter_context(nc.Block())

        @block.sync
        def _(sp):
            sp.dma_start(x_all[:, 0:S], x[0, :, :]).then_inc(x0_in, 16)
            sp.dma_start(wkv_sb[:, :], w_kv).then_inc(kv_in, 16)
            sp.dma_start(ctx_sb[:, :], ctx_t).then_inc(kv_in, 16)
            sp.dma_start(vec[:, :], vecs).then_inc(kv_in, 16)
            sp.dma_start(cst[:, :], consts).then_inc(attn_in, 16)
            sp.dma_start(wq_sb[:, :], w_q).then_inc(attn_in, 16)
            sp.dma_start(x_all[:, S:B * S].rearrange("p (b n) -> p b n", b=B - 1),
                         x[1:B, :, :].rearrange("b p n -> p b n")).then_inc(x_in, 16)
            sp.dma_start(wo_sb[:, :], w_out).then_inc(wo_in, 16)
            sp.dma_start(w1_sb[:, 0:(E + 1) * HID], w1).then_inc(ffn_in, 16)
            sp.dma_start(w3_sb[:, 0:(E + 1) * HID], w3).then_inc(ffn_in, 16)
            sp.dma_start(w2_sb[:, 0:FP - D], w2[:, 0:FP - D]).then_inc(ffn_in, 16)
            last = (E + 1) * HID - (NFC - 1) * P
            sp.wait_ge(pads, 5)
            sp.dma_start(w2_sb[0:last, FP - D:FP], w2[0:last, FP - D:FP]).then_inc(ffn_in, 16)
            sp.dma_start(gw_sb[:, 0:E], gate_wt).then_inc(ffn_in, 16)
            for q in range(3):
                sp.dma_start(b2_sb[32 * q:32 * q + E + 1, :], b2).then_inc(ffn_in, 16)
            for q in range(2):
                sp.dma_start(sel_sb[32 * q:32 * q + E, :], sel_rows).then_inc(ffn_in, 16)

            def place_values(batches, done):
                n = len(batches)
                src = v_sb[:, batches[0] * D:(batches[-1] + 1) * D].rearrange("p (b n) -> p b n", b=n)
                for c, h, r0, r1 in PIECES:
                    sp.dma_start(vw4[r0 - c * P:r1 - c * P, batches[0]:batches[-1] + 1, c, h * VC:h * VC + HD],
                                 src[r0 - h * Z:r1 - h * Z, :, h * HD:(h + 1) * HD]).then_inc(done, 16)

            sp.wait_ge(v_moved, 1)
            sp.wait_ge(vw_zero, 1)
            place_values(range(1), vw_in)
            sp.wait_ge(vw_zero_rest, 1)
            place_values(range(1, B), vw_rest_in)

            def fetch(b):
                sp.wait_ge(ln1_done, b * NT + NT)
                sp.wait_ge(xt_ps_ready, b)
                sp.dma_start(xn1[:, :], x_all[:, bass.ds(b * S, S)]).then_inc(xn1_in, 16)

            def store(b):
                sp.wait_ge(y_moved, b + 2)
                sp.dma_start(out[b, :, :], y_sb[:, :]).then_inc(out_done, 16)

            fetch(1)
            with sp.Fori(2, B) as b:
                fetch(b)
                store(b - 2)
            store(B - 2)
            store(B - 1)
            sp.wait_ge(out_done, 16 * (B + 1))

        @block.gpsimd
        def _(pool):
            pool.memset(mhalf[:, :], -0.5).then_inc(pads, 1)
            for pad in (w2_sb[:, FP - D:FP], b2_sb[:, :], sel_sb[:, :], gw_sb[:, :], w1_sb[:, (E + 1) * HID:FP],
                        w3_sb[:, (E + 1) * HID:FP], lg[0][:, HZ:HZP], lg[1][:, HZ:HZP], rw[:, :]):
                pool.memset(pad, 0.0).then_inc(pads, 1)
            pool.wait_ge(pads, 10)
            for q in (0, 2):
                pool.memset(rw3[:, :, 32 * q + E:32 * q + E + 1], 1.0).then_inc(pads, 1)

            def rstd_step(out_, in_):
                return pool.tensor_tensor(out_, in_, mhalf[:, 0:in_.shape[1]], ALU.pow)

            def rstd2_step(a):
                pool.wait_ge(ln2_eps, a + 1)
                rstd_step(rstd2[:, :], veps2[:, :]).then_inc(ln2_rstd, 1)

            def keys(a):
                pool.wait_ge(mx_ready, 2 * NT * a + 1)
                spread_keys(pool, kb_hi, k_hi, a).then_inc(kb_ready, 1)
                spread_keys(pool, kb_lo, k_lo, a).then_inc(kb_ready, 1)

            def lower_weights(i, lo, w, hi):
                pool.wait_ge(w_his, i)
                pool.tensor_tensor(lo[:, :], w[:, :], hi[:, :].bitcast(f32), ALU.subtract).then_inc(w_split, 1)

            def multiply(f, n):
                pool.wait_ge(p_ready, f * NFC + n + 3)
                pool.wait_ge(rb_moved, f * len(AIDED) + before(AIDED, n) + 2)
                pool.wait_ge(h_ready, f * NFC + n - 1)
                pool.tensor_tensor(pr_sb[n % 2][:, :], rb_sb[:, :], p_sb[n % 2][:, :], ALU.mult).then_inc(pr_aided, 1)

            def lower(f, n):
                k = f * NFC + n
                pool.wait_ge(h_hi_ready, f * len(SPLIT) + before(SPLIT, n) + 1)
                pool.wait_ge(down_done, k + 1)
                pool.tensor_tensor(h_lo[n % 3][:, :], h_sb[h_slot(n)][:, :], h_hi[n % 3][:, :].bitcast(f32),
                                   ALU.subtract).then_inc(h_lo_ready, 1)

            def first():
                pool.wait_ge(ln1_eps, 1)
                rstd_step(rstd1[:, 0:NT], veps1[:, 0:NT]).then_inc(ln1_rstd, 1)
                pool.wait_ge(attn_in, 16 * N_ATTN_IN)
                pool.wait_ge(k_split, 1)
                spread_keys(pool, kb_hi, k_hi, 0).then_inc(kb_ready, 1)
                pool.memset(vw[:, NZC * VW_W:B * NZC * VW_W], 0.0).then_inc(vw_zero_rest, 1)
                pool.wait_ge(x_in, 16)
                pool.wait_ge(x0_in, 16)
                pool.tensor_tensor(xb_all[:, :].rearrange("p (t d) -> p t d", d=D),
                                   x_all[:, :].rearrange("p (t d) -> p t d", d=D),
                                   vec[:, V_BO:V_BO + D].unsqueeze(1).broadcast_to([P, B * NT, D]),
                                   ALU.add).then_inc(xb_ready, 1)
                third = slice(64, 96)
                pool.wait_ge(w_his, 1)
                pool.wait_ge(xb_ready, 1)
                pool.tensor_tensor(b2_st[third, :], b2_sb[third, :], b2_st[third, :].bitcast(f32), ALU.subtract).then_inc(w_split, 1)
                pool.wait_ge(w_split, 1)
                lower_weights(2, w1_lo, w1_sb, w1_hi)
                pool.wait_ge(ln1_eps, 2)
                rstd_step(rstd1[:, NT:B * NT], veps1[:, NT:B * NT]).then_inc(ln1_rstd, 1)
                lower_weights(3, w3_lo, w3_sb, w3_hi)
                rstd2_step(0)

            def both(a, f):
                keys(a)
                multiply(f, 2)
                for n in SPLIT:
                    lower(f, n)
                multiply(f, 8)
                multiply(f, 9)
                rstd2_step(a)
                multiply(f, 10)
                multiply(f, 11)

            def last(f):
                for n in range(NFC):
                    if n in AIDED:
                        multiply(f, n)
                    if n in SPLIT:
                        lower(f, n)

            pipeline(pool, first, both, last)

        @block.scalar
        def _(act):
            for s, credit in ((pt_moved, 1), (u_moved, 1), (y_moved, 1), (out_done, 16)):
                act.sem_inc(s, credit)
            act.wait_ge(k_proj, 1)
            act.activation(k_f[:, :], ps_t[:, 0:B * Z], ACT.Identity, bias=bk).then_inc(k_bias, 1)

            def small_weights():
                act.wait_ge(ffn_in, 16 * N_FFN_IN)
                act.wait_ge(pads, N_PADS)
                act.activation(w2_sb[:, NEC * P:FP], w2_sb[:, NEC * P:FP], ACT.Copy, scale=0.5).then_inc(w2_half, 1)
                act.activation(b2_st[:, :], b2_sb[:, :], ACT.Copy).then_inc(w_his, 1)

            def upper_weights(hi, w):
                act.activation(hi[:, :], w[:, :], ACT.Copy).then_inc(w_his, 1)

            def normalise_2(a):
                act.wait_ge(ln2_shift, a)
                for t in range(NT):
                    act.activation(tile_of(xn2, t), tile_of(x1, t), ACT.Identity,
                                   bias=nmr2[:, t:t + 1], scale=rstd2[:, t:t + 1]).then_inc(xn2_ready, 1)

            def move_xt(a):
                act.wait_ge(xt_ps_ready, a + 1)
                act.activation(xt[:, :], ps_t[:, :], ACT.Copy).then_inc(xt_ready, 1)

            def q_upper(a):
                act.wait_ge(q_ps_ready, a + 1)
                act.activation(q_hi[:, :], ps_m[:, :], ACT.Identity, bias=bq).then_inc(q_hi_ready, 1)

            def move_values():
                act.wait_ge(vp_ready, 1)
                act.activation(v_sb[0:Z, :], ps_v[0:Z, :], ACT.Copy).then_inc(v_moved, 1)

            def exps(a, half):
                t, g = divmod(half, 2)
                part = lg[t % 2][:, g * HALF:(g + 1) * HALF]
                act.wait_ge(lg_sub, a * 2 * NT + half + 2)
                act.activation(part, part, ACT.Exp).then_inc(exp_done, 1)

            def move_pt(a, t, g, f):
                cols = min(BANK, HZP - g * BANK)
                act.wait_ge(pt_ps_ready, a * 3 * NT + 3 * t + g + 1)
                if t >= 2 and g == 0:
                    act.wait_ge(av_ready, a * NT + t - 1)
                act.activation(pt[t % 2][:, g * BANK:g * BANK + cols], turn_bank(f, g)[:, 0:cols], ACT.Copy).then_inc(pt_moved, 1)

            def move_aot(a):
                act.wait_ge(aot_ps_ready, a + 1)
                act.activation(aot[:, :], ps_t[:, :], ACT.Identity, bias=bv).then_inc(aot_ready, 1)

            def move_x2(a):
                act.wait_ge(x2_ps_ready, a + 1)
                act.activation(x2t[:, :], ps_t[:, :], ACT.Copy).then_inc(x2_ready, 1)

            def x2_upper(f):
                act.wait_ge(x2_ps_ready, f + 1)
                act.wait_ge(v_ready, f * NFC + 1)
                act.activation(x2t_hi[:, :], ps_t[:, :], ACT.Copy).then_inc(x2_hi_ready, 1)

            def router_exp(f):
                act.wait_ge(gsub_ready, f + 1)
                act.activation(ge[:, :], ge[:, :], ACT.Exp).then_inc(gexp_ready, 1)

            def move_rwt(f):
                act.wait_ge(rwt_ps_ready, f + 1)
                act.activation(rwt[:, :], ps_t[:, :], ACT.Copy).then_inc(rwt_ready, 1)

            def u_step(f, n):
                k, c = f * NFC + n, CHUNKS[n]
                act.wait_ge(u_ready, k + 1)
                act.wait_ge(p_ready, k + 1)
                act.activation(u_sb[n % 2][:, :], ps_u[:, :], ACT.Identity, bias=vec[:, V_B1 + c:V_B1 + c + 1]) \
                    .then_inc(u_moved, 1)

            def move_rb(f, n):
                if n not in AIDED:
                    return
                e = f * NEC + n - NSH
                act.wait_ge(rb_ready, e + 1)
                act.wait_ge(pr_aided, f * len(AIDED) + before(AIDED, n) + 1)
                act.activation(rb_sb[:, :], ps_rb[:, :], ACT.Copy).then_inc(rb_moved, 1)

            def tanh_step(f, n):
                act.wait_ge(p_ready, f * NFC + n + 3)
                act.activation(t_sb[n % 2][:, :], p_sb[n % 2][:, :], ACT.Tanh, scale=0.5).then_inc(t_ready, 1)

            def upper(f, n):
                if n not in SPLIT:
                    return
                k = f * NFC + n
                act.wait_ge(h_ready, k + 1)
                act.wait_ge(down_done, k + 1)
                act.activation(h_hi[n % 3][:, :], h_sb[h_slot(n)][:, :], ACT.Copy).then_inc(h_hi_ready, 1)

            def move_y(f):
                act.wait_ge(down_done, f * NFC + NFC + 3)
                act.wait_ge(out_done, 16 * f + 16)
                act.activation(y_sb[:, :], ps_y[:, :], ACT.Copy).then_inc(y_moved, 1)

            def first():
                def move_tile(t):
                    for g in range(3):
                        move_pt(0, t, g, None)

                move_values()
                move_xt(0)
                q_upper(0)
                exps(0, 0)
                exps(0, 1)
                exps(0, 2)
                exps(0, 3)
                move_tile(0)
                exps(0, 4)
                move_tile(1)
                exps(0, 5)
                small_weights()
                exps(0, 6)
                upper_weights(w1_hi, w1_sb)
                move_tile(2)
                exps(0, 7)
                upper_weights(w3_hi, w3_sb)
                move_tile(3)
                upper_weights(sel, sel_sb)
                move_aot(0)
                move_x2(0)
                x2_upper(0)
                u_step(0, 0)
                router_exp(0)
                tanh_step(0, 0)

            def both(a, f):
                move_xt(a)
                u_step(f, 1)
                q_upper(a)
                u_step(f, 2)
                tanh_step(f, 1)
                tanh_step(f, 2)
                u_step(f, 3)
                move_rwt(f)
                exps(a, 0)
                move_rb(f, 2)
                tanh_step(f, 3)
                exps(a, 1)
                for t in range(NT):
                    n = 4 + t
                    u_step(f, n)
                    move_pt(a, t, 0, f)
                    move_pt(a, t, 1, f)
                    upper(f, n - 1)
                    if t < NT - 1:
                        exps(a, 2 * t + 2)
                    move_pt(a, t, 2, f)
                    tanh_step(f, n)
                    if t < NT - 1:
                        exps(a, 2 * t + 3)
                u_step(f, 8)
                upper(f, 7)
                move_aot(a)
                u_step(f, 9)
                tanh_step(f, 8)
                for n in range(9, NFC):
                    if n > 9:
                        u_step(f, n)
                    if n == 11:
                        tanh_step(f, 10)
                    move_rb(f, n - 1)
                    if n == 11:
                        normalise_2(a)
                    if n == 12:
                        move_x2(a)
                        x2_upper(a)
                    if n != 10:
                        tanh_step(f, n)
                u_step(a, 0)
                router_exp(a)
                tanh_step(a, 0)
                move_y(f)

            def last(f):
                for n in range(1, NFC):
                    if n == NFC - 1:
                        move_rb(f, n - 1)
                    u_step(f, n)
                    upper(f, n - 1)
                    if n == 3:
                        move_rwt(f)
                    if 3 < n < NFC - 1:
                        move_rb(f, n - 1)
                    tanh_step(f, n)
                    if n == 3:
                        move_rb(f, 2)
                move_y(f)

            pipeline(act, first, both, last)

        @block.vector
        def _(dve):
            for s, credit in ((lg_sub, 1), (mx_ready, 1), (p_ready, 2), (pr_ready, 1), (down_done, 3), (rb_moved, 1), (pr_aided, 1)):
                dve.sem_inc(s, credit)

            def stats1_step(tiles):
                for t in tiles:
                    dve.bn_stats(stats1[:, 6 * t:6 * t + 6], tile_of(x_all, t)).then_inc(ln1_stats, 1)

            def ln1(tiles):
                for t in tiles:
                    dve.wait_ge(ln1_stats, t + 1)
                    dve.bn_aggr(mv1[:, 2 * t:2 * t + 2], stats1[:, 6 * t:6 * t + 6]).then_inc(ln1_mv, 1)
                t0, t1 = tiles[0], tiles[-1] + 1
                dve.wait_ge(ln1_mv, t1)
                dve.tensor_scalar(veps1[:, t0:t1], mv1[:, 2 * t0:2 * t1].rearrange("p (t s) -> p t s", s=2)[:, :, 1], EPS, None,
                                  ALU.add).then_inc(ln1_eps, 1)

            def normalise1(part, tiles):
                dve.wait_ge(ln1_rstd, part + 1)
                if part == 1:
                    dve.wait_ge(xb_ready, 1)
                for t in tiles:
                    dve.tensor_scalar(tile_of(xn1 if part == 0 else x_all, t), tile_of(x_all, t), mv1[:, 2 * t:2 * t + 1],
                                      rstd1[:, t:t + 1], ALU.subtract, ALU.mult).then_inc(ln1_done, 1)

            def q_lower(a):
                dve.wait_ge(q_hi_ready, a + 1)
                dve.scalar_tensor_tensor(q_lo[:, :], ps_m[:, :], bq, q_hi[:, :].bitcast(f32),
                                         ALU.add, ALU.subtract).then_inc(q_lo_ready, 1)

            def logits(a, half, f):
                t, g = divmod(half, 2)
                k = a * 2 * NT + half
                dst = lg[t % 2][:, g * HALF:(g + 1) * HALF].rearrange("p (a h z) -> p a h z", a=2, z=Z)
                m = mx[:, g * 8:g * 8 + 8].rearrange("p (a h) -> p a h", a=2)
                src = lg_banks(f, half)[:, :].rearrange("p (a n) -> p a n", a=2)[:, :, 0:QUART].rearrange("p a (h z) -> p a h z", z=Z)
                dve.wait_ge(lg_ready, k + 1)
                if half >= 4:
                    dve.wait_ge(pt_ps_ready, a * 3 * NT + 3 * (t - 1))
                if t == 0:
                    dve.tensor_tensor(dst, src, cst[:, C_TRI:C_TRI + Z].unsqueeze(1).unsqueeze(1).broadcast_to([P, 2, 4, Z]),
                                      ALU.subtract).then_inc(lg_masked, 1)
                    src = dst
                    dve.wait_ge(lg_masked, 2 * a + g + 1)
                dve.tensor_reduce(m, src, AX, ALU.max).then_inc(mx_ready, 1)
                dve.wait_ge(mx_ready, k + 2)
                dve.tensor_tensor(dst, src, m.unsqueeze(3).broadcast_to([P, 2, 4, Z]), ALU.subtract).then_inc(lg_sub, 1)

            def normalise(a, pr):
                src = ps_m[:, 0:2 * VW_W].rearrange("p (t h v) -> p t h v", t=2, v=VC)
                rd = rden[:, :].rearrange("p (t h) -> p t h", t=2)
                dve.wait_ge(av_ready, a * NT + 2 * pr + 2)
                dve.reciprocal(rd, src[:, :, :, HD]).then_inc(rden_ready, 1)
                dve.wait_ge(rden_ready, 2 * a + pr + 1)
                dve.tensor_tensor(ao[:, 2 * pr * P:2 * (pr + 1) * P].rearrange("p (t h v) -> p t h v", t=2, v=HD),
                                  src[:, :, :, 0:HD], rd.unsqueeze(3).broadcast_to([P, 2, HEADS, HD]),
                                  ALU.mult).then_inc(ao_ready, 1)

            def residual(a):
                dve.wait_ge(proj_ready, a + 1)
                dve.wait_ge(xb_ready, 1)
                dve.tensor_tensor(x1[:, :], ps_m[:, :], xb_all[:, bass.ds(a * S, S)], ALU.add).then_inc(x1_ready, 1)

            def stats2_step(a):
                dve.wait_ge(x1_ready, a + 1)
                for t in range(NT):
                    dve.bn_stats(stats2[:, 6 * t:6 * t + 6], tile_of(x1, t)).then_inc(ln2_stats, 1)

            def ln2(a):
                dve.wait_ge(ln2_stats, a * NT + NT)
                dve.memset(spare[:, :], 0.0)
                for t in range(NT):
                    dve.bn_aggr(mv2[:, 2 * t:2 * t + 2], stats2[:, 6 * t:6 * t + 6]).then_inc(ln2_mv, 1)
                dve.wait_ge(ln2_mv, a * NT + NT)
                dve.tensor_scalar(veps2[:, :], mv2[:, :].rearrange("p (t s) -> p t s", s=2)[:, :, 1], EPS, None,
                                  ALU.add).then_inc(ln2_eps, 1)

            def normalise2(a):
                dve.wait_ge(ln2_rstd, a + 1)
                for t in range(NT):
                    dve.tensor_scalar(tile_of(xn2, t), tile_of(x1, t), mv2[:, 2 * t:2 * t + 1], rstd2[:, t:t + 1],
                                      ALU.subtract, ALU.mult).then_inc(xn2_ready, 1)

            def shift2(a):
                dve.wait_ge(ln2_rstd, a + 1)
                dve.scalar_tensor_tensor(nmr2[:, :], mv2[:, :].rearrange("p (t s) -> p t s", s=2)[:, :, 0], -1.0,
                                         rstd2[:, :], ALU.mult, ALU.mult).then_inc(ln2_shift, 1)

            def x2_lower(f):
                dve.wait_ge(x2_hi_ready, f + 1)
                dve.tensor_tensor(x2t_lo[:, :], ps_t[:, :], x2t_hi[:, :].bitcast(f32), ALU.subtract).then_inc(x2_lo_ready, 1)

            LINKS = 12

            def link(f, i, ins):
                ins.then_inc(gchain, 1)
                dve.wait_ge(gchain, f * LINKS + i)

            def per_token(ap):
                return ap[:, :].unsqueeze(2).broadcast_to([P, NT, E])

            def tok(ap):
                return ap[:, :].rearrange("p (t e) -> p t e", t=NT)

            def router_scores(f):
                scores = ps_m[:, 0:NT * GW].rearrange("p (t n) -> p t n", t=NT)[:, :, 0:E]
                dve.wait_ge(gate_ready, f + 1)
                link(f, 1, dve.tensor_reduce(gmax[:, :], scores, AX, ALU.max))
                dve.tensor_tensor(tok(ge), scores, per_token(gmax), ALU.subtract).then_inc(gsub_ready, 1)

            def router_softmax(f):
                dve.wait_ge(gexp_ready, f + 1)
                link(f, 2, dve.tensor_reduce(gsum[:, :], tok(ge), AX, ALU.add))
                link(f, 3, dve.reciprocal(grec[:, :], gsum[:, :]))
                link(f, 4, dve.tensor_tensor(tok(gs), tok(ge), per_token(grec), ALU.mult))
                link(f, 5, dve.tensor_tensor(tok(gbias), tok(gs),
                                             vec[:, V_GB:V_GB + E].unsqueeze(1).broadcast_to([P, NT, E]), ALU.add))

            def router_compare(f):
                mine = tok(gbias).unsqueeze(3).broadcast_to([P, NT, E, E])
                others = tok(gbias).unsqueeze(2).broadcast_to([P, NT, E, E])
                dve.tensor_tensor(cgt[:, :].rearrange("p (t e f) -> p t e f", e=E, f=E), others, mine, ALU.is_gt)
                last = dve.tensor_tensor(ceq[:, :].rearrange("p (t e f) -> p t e f", e=E, f=E), others, mine, ALU.is_equal)
                last.then_inc(gchain, 1)

            def router_rank(f):
                dve.wait_ge(gchain, f * LINKS + 6)
                eqt = ceq[:, :].rearrange("p (t n) -> p t n", t=NT)
                link(f, 7, dve.tensor_tensor(eqt, eqt, cst[:, C_LT:C_LT + E * E].unsqueeze(1).broadcast_to([P, NT, E * E]), ALU.mult))
                link(f, 8, dve.tensor_tensor(cgt[:, :], cgt[:, :], ceq[:, :], ALU.add))

            def router_choose(f):
                link(f, 9, dve.tensor_reduce(rank[:, :], cgt[:, :].rearrange("p (n f) -> p n f", f=E), AX, ALU.add))
                link(f, 10, dve.tensor_scalar(chosen[:, :], rank[:, :], 2.0, None, ALU.is_lt))
                link(f, 11, dve.tensor_tensor(tok(gs), tok(gs), tok(chosen), ALU.mult))
                link(f, 12, dve.tensor_copy(rw_hi[:, :], gs[:, :]))
                hi = tok(rw_hi).bitcast(f32)
                dve.tensor_copy(rw3[:, :, 0:E], hi)
                dve.tensor_copy(rw3[:, :, 64:64 + E], hi)
                dve.tensor_tensor(rw3[:, :, 32:32 + E], tok(gs), hi, ALU.subtract).then_inc(rw_ready, 1)

            def p_step(f, n):
                k, c = f * NFC + n, CHUNKS[n]
                dve.wait_ge(v_ready, k + 2)
                dve.wait_ge(u_moved, k + 2)
                if n >= 2:
                    dve.wait_ge(t_ready, k - 1)
                    if not routed(n - 2):
                        dve.wait_ge(h_ready, k - 1)
                dve.scalar_tensor_tensor(p_sb[n % 2][:, :], ps_v[:, :], vec[:, V_B3 + c:V_B3 + c + 1],
                                         u_sb[n % 2][:, :], ALU.add, ALU.mult).then_inc(p_ready, 1)

            def multiply(f, n):
                if n in ALONE:
                    k, e = f * NFC + n, f * NEC + n - NSH
                    dve.wait_ge(h_ready, k - 1)
                    dve.wait_ge(p_ready, k + 3)
                    dve.wait_ge(rb_ready, e + 1)
                    dve.tensor_tensor(pr_sb[n % 2][:, :], ps_rb[:, :], p_sb[n % 2][:, :], ALU.mult).then_inc(pr_ready, 1)

            def gate(f, n):
                k, src = f * NFC + n, p_sb[n % 2]
                if n in ALONE:
                    dve.wait_ge(pr_ready, f * len(ALONE) + before(ALONE, n) + 2)
                if n in AIDED:
                    dve.wait_ge(pr_aided, f * len(AIDED) + before(AIDED, n) + 2)
                if routed(n):
                    src = pr_sb[n % 2]
                dve.wait_ge(t_ready, k + 1)
                dve.wait_ge(down_done, k + 1)
                dve.scalar_tensor_tensor(h_sb[h_slot(n)][:, :], t_sb[n % 2][:, :], 1.0, src[:, :],
                                         ALU.add, ALU.mult).then_inc(h_ready, 1)

            def first():
                dve.memset(vw[:, 0:NZC * VW_W], 0.0).then_inc(vw_zero, 1)
                dve.wait_ge(x0_in, 16)
                stats1_step(range(0, NT))
                ln1(range(0, NT))
                normalise1(0, range(0, NT))
                dve.wait_ge(k_bias, 1)
                dve.tensor_copy(k_hi[:, :], k_f[:, :]).then_inc(k_split, 1)
                dve.wait_ge(k_split, 1)
                dve.tensor_tensor(k_lo[:, :], k_f[:, :], k_hi[:, :].bitcast(f32), ALU.subtract).then_inc(k_split, 1)
                dve.wait_ge(attn_in, 16 * N_ATTN_IN)
                dve.wait_ge(k_split, 2)
                spread_keys(dve, kb_lo, k_lo, 0).then_inc(kb_lo_ready, 1)
                q_lower(0)
                logits(0, 0, None)
                logits(0, 1, None)
                logits(0, 2, None)
                dve.wait_ge(vw_zero_rest, 1)
                dve.wait_ge(vw_zero, 1)
                dve.tensor_copy(vw[:, :].rearrange("p (b n v) -> p b n v", b=B, v=VC)[:, :, :, HD],
                                cst[:, C_ZM:C_ZM + NZC * HEADS].unsqueeze(1).broadcast_to([P, B, NZC * HEADS])).then_inc(ones_ready, 1)
                logits(0, 3, None)
                logits(0, 4, None)
                logits(0, 5, None)
                logits(0, 6, None)
                logits(0, 7, None)
                dve.wait_ge(x_in, 16)
                stats1_step(range(NT, B * NT))
                ln1(range(NT, B * NT))
                normalise(0, 0)
                dve.wait_ge(w2_half, 1)
                dve.tensor_copy(w2_hi[:, :], w2_sb[:, :]).then_inc(w2_split, 1)
                dve.wait_ge(w2_split, 1)
                dve.tensor_tensor(w2_lo[:, :], w2_sb[:, :], w2_hi[:, :].bitcast(f32), ALU.subtract).then_inc(w2_split, 1)
                normalise(0, 1)
                normalise1(1, range(NT, B * NT))
                residual(0)
                stats2_step(0)
                ln2(0)
                normalise2(0)
                x2_lower(0)
                router_scores(0)
                p_step(0, 0)

            def both(a, f):
                router_softmax(f)
                router_compare(f)
                gate(f, 0)
                p_step(f, 1)
                router_rank(f)
                q_lower(a)
                p_step(f, 2)
                router_choose(f)
                logits(a, 0, f)
                gate(f, 1)
                p_step(f, 3)
                logits(a, 1, f)
                gate(f, 2)
                for t in range(NT):
                    n = 4 + t
                    if t == 2:
                        normalise(a, 0)
                    multiply(f, n - 1)
                    gate(f, n - 1)
                    if t < NT - 1:
                        logits(a, 2 * t + 2, f)
                    p_step(f, n)
                    if t < NT - 1:
                        logits(a, 2 * t + 3, f)
                normalise(a, 1)
                multiply(f, 7)
                gate(f, 7)
                p_step(f, 8)
                p_step(f, 9)
                residual(a)
                stats2_step(a)
                gate(f, 8)
                ln2(a)
                p_step(f, 10)
                shift2(a)
                gate(f, 9)
                p_step(f, 11)
                gate(f, 10)
                p_step(f, 12)
                x2_lower(a)
                gate(f, 11)
                multiply(f, 12)
                gate(f, 12)
                router_scores(a)
                p_step(a, 0)

            def last(f):
                router_softmax(f)
                router_compare(f)
                gate(f, 0)
                p_step(f, 1)
                router_rank(f)
                router_choose(f)
                p_step(f, 2)
                gate(f, 1)
                p_step(f, 3)
                gate(f, 2)
                for n in range(4, NFC):
                    if n - 1 in ALONE:
                        multiply(f, n - 1)
                        gate(f, n - 1)
                    p_step(f, n)
                    if n - 1 in AIDED:
                        gate(f, n - 1)
                multiply(f, NFC - 1)
                gate(f, NFC - 1)

            pipeline(dve, first, both, last)

        @block.tensor
        def _(pe):
            pe.sem_inc(v_ready, 1)

            def three(dst, hi, lo, mhi, mlo, start=True, stop=True):
                pe.matmul(dst, hi, mhi, start=start, stop=False)
                pe.matmul(dst, hi, mlo, start=False, stop=False)
                return pe.matmul(dst, lo, mhi, start=False, stop=stop)

            def transposes(src):
                for t in range(NT):
                    last = pe.transpose(tile_of(ps_t, t), tile_of(src, t), ident)
                return last

            pe.wait_ge(kv_in, 16 * N_KV_IN)
            pe.matmul(ps_t[:, 0:B * Z], wkv_sb[:, 0:D], ctx_sb[:, :], start=True, stop=True).then_inc(k_proj, 1)
            for b in range(B):
                last = pe.matmul(ps_v[0:Z, b * D:(b + 1) * D], ctx_sb[:, b * Z:(b + 1) * Z], wkv_sb[:, D:2 * D], start=True, stop=True)
            last.then_inc(vp_ready, 1)
            pe.wait_ge(k_bias, 1)

            def turn_x(a):
                if type(a) is int:
                    pe.wait_ge(attn_in, 16 * N_ATTN_IN)
                    pe.wait_ge(ln1_done, NT)
                else:
                    pe.wait_ge(xn1_in, 16 * a)
                transposes(xn1).then_inc(xt_ps_ready, 1)

            def queries(a, f):
                pe.wait_ge(xt_ready, a + 1)
                if f is not None:
                    pe.wait_ge(gsub_ready, f + 1)
                pe.matmul(ps_m[:, :], wq_sb[:, :], xt[:, :], start=True, stop=True).then_inc(q_ps_ready, 1)

            def logits(a, half, f):
                t, g = divmod(half, 2)
                k = a * 2 * NT + half
                if half == 0:
                    if f is None:
                        pe.wait_ge(kb_ready, 1)
                        pe.wait_ge(kb_lo_ready, 1)
                    else:
                        pe.wait_ge(kb_ready, 2 * a + 1)
                    pe.wait_ge(q_hi_ready, a + 1)
                    pe.wait_ge(q_lo_ready, a + 1)
                if f is not None:
                    pe.wait_ge(lg_sub, k + 1)
                elif half >= 2:
                    pe.wait_ge(lg_sub, k)
                for i in range(2):
                    cols = slice(g * HALF + i * QUART, g * HALF + (i + 1) * QUART)
                    last = three(lg_banks(f, half)[:, i * BANK:i * BANK + QUART], tile_of(q_hi, t), tile_of(q_lo, t), kb_hi[:, cols], kb_lo[:, cols])
                last.then_inc(lg_ready, 1)

            def turn_probs(a, t, g, f):
                k = a * 3 * NT + 3 * t + g
                if g < 2:
                    pe.wait_ge(exp_done, a * 2 * NT + 2 * t + 1 + g)
                if g == 0:
                    if t == 0:
                        if f is None:
                            pe.wait_ge(xt_ready, 1)
                        else:
                            pe.wait_ge(rwt_ready, f + 1)
                if f is not None:
                    pe.wait_ge(pt_moved, k + 1)
                elif t > 0:
                    pe.wait_ge(pt_moved, k - 1)
                for c in group(g):
                    last = pe.transpose(tile_of(turn_bank(f, g), c - 4 * g), tile_of(lg[t % 2], c), ident)
                last.then_inc(pt_ps_ready, 1)

            def weigh(a, t, f):
                pe.wait_ge(pt_moved, a * 3 * NT + 3 * t + 3)
                if t == 0:
                    if f is None:
                        pe.wait_ge(vw_in, 16 * len(PIECES))
                    else:
                        pe.wait_ge(vw_rest_in, 16 * len(PIECES))
                    pe.wait_ge(ones_ready, 1)
                if t == 2:
                    pe.wait_ge(ao_ready, 2 * a + 1)
                o = (t % 2) * VW_W
                for c in range(NZC):
                    w0 = 0 if c == 0 else min(c * P // Z, HEADS - WIN_HEADS) * VC
                    w1_ = VW_W if c == 0 else w0 + WIN_HEADS * VC
                    if c == group(2)[0]:
                        pe.wait_ge(pt_moved, a * 3 * NT + 3 * t + 4)
                    last = pe.matmul(ps_m[:, o + w0:o + w1_], tile_of(pt[t % 2], c),
                                     vw[:, bass.ds((a * NZC + c) * VW_W + w0, w1_ - w0)], start=(c == 0), stop=(c == NZC - 1))
                last.then_inc(av_ready, 1)

            def turn_ao(a):
                pe.wait_ge(ao_ready, 2 * a + 2)
                transposes(ao).then_inc(aot_ps_ready, 1)

            def project(a):
                pe.wait_ge(aot_ready, a + 1)
                pe.wait_ge(wo_in, 16)
                for t in range(NT):
                    last = pe.matmul(tile_of(ps_m, t), tile_of(aot, t), wo_sb[:, :], start=True, stop=True)
                last.then_inc(proj_ready, 1)

            def turn_x2(a):
                pe.wait_ge(xn2_ready, a * NT + NT)
                transposes(xn2).then_inc(x2_ps_ready, 1)

            def router(a):
                pe.wait_ge(x2_ready, a + 1)
                pe.wait_ge(ffn_in, 16 * N_FFN_IN)
                for t in range(NT):
                    last = pe.matmul(ps_m[:, t * GW:(t + 1) * GW], tile_of(x2t, t), gw_sb[:, :], start=True, stop=True)
                last.then_inc(gate_ready, 1)

            def up_u(f, n):
                k, c = f * NFC + n, CHUNKS[n]
                pe.wait_ge(u_moved, k + 1)
                three(ps_u[:, :], tile_of(w1_hi, c), tile_of(w1_lo, c), x2t_hi[:, :], x2t_lo[:, :]).then_inc(u_ready, 1)

            def up_v(f, n):
                k, c = f * NFC + n, CHUNKS[n]
                pe.wait_ge(p_ready, k + 2)
                three(ps_v[:, :], tile_of(w3_hi, c), tile_of(w3_lo, c), x2t_hi[:, :], x2t_lo[:, :]).then_inc(v_ready, 1)

            def spread(f, n):
                if n == NSH:
                    pe.wait_ge(rwt_ready, f + 1)
                if n - 1 in AIDED:
                    pe.wait_ge(rb_moved, f * len(AIDED) + before(AIDED, n - 1) + 2)
                else:
                    pe.wait_ge(pr_ready, f * len(ALONE) + before(ALONE, n) + 1)
                pe.matmul(ps_rb[:, :], tile_of(sel, CHUNKS[n]), rwt[:, :], start=True, stop=True).then_inc(rb_ready, 1)

            def down(f, n, start=False, stop=False):
                c = CHUNKS[n]
                if start:
                    pe.wait_ge(y_moved, f + 1)
                if n in SPLIT:
                    pe.wait_ge(h_lo_ready, f * len(SPLIT) + before(SPLIT, n) + 1)
                else:
                    pe.wait_ge(h_ready, f * NFC + n + 1)
                    return pe.matmul(ps_y[:, :], tile_of(w2_sb, c), h_sb[h_slot(n)][:, :], start=start, stop=stop).then_inc(down_done, 1)
                return three(ps_y[:, :], tile_of(w2_hi, c), tile_of(w2_lo, c), h_hi[n % 3][:, :], h_lo[n % 3][:, :],
                             start=start, stop=stop).then_inc(down_done, 1)

            def bias_and_residual(f):
                pe.wait_ge(rwt_ready, f + 1)
                pe.matmul(ps_y[:, :], b2_st[:, :], rwt[:, :], start=False, stop=False)
                for t in range(NT):
                    pe.matmul(tile_of(ps_y, t), tile_of(x1, t), ident, start=False, stop=False)

            def turn_rw(a, f):
                pe.wait_ge(rw_ready, f + 1)
                if a is not None:
                    pe.wait_ge(xt_ready, a + 1)
                transposes(rw).then_inc(rwt_ps_ready, 1)

            def first():
                def turn_tile(t):
                    for g in range(3):
                        turn_probs(0, t, g, None)

                turn_x(0)
                queries(0, None)
                logits(0, 0, None)
                logits(0, 1, None)
                logits(0, 2, None)
                logits(0, 3, None)
                turn_tile(0)
                logits(0, 4, None)
                logits(0, 5, None)
                turn_tile(1)
                logits(0, 6, None)
                weigh(0, 0, None)
                logits(0, 7, None)
                turn_tile(2)
                weigh(0, 1, None)
                turn_tile(3)
                weigh(0, 2, None)
                weigh(0, 3, None)
                turn_ao(0)
                project(0)
                turn_x2(0)
                start_up(0)

            def start_up(a):
                router(a)
                pe.wait_ge(w_split, 3)
                pe.wait_ge(w_his, 4)
                pe.wait_ge(w2_split, 2)
                pe.wait_ge(x2_hi_ready, a + 1)
                pe.wait_ge(x2_lo_ready, a + 1)
                up_u(a, 0)
                up_v(a, 0)

            def both(a, f):
                turn_x(a)
                up_u(f, 1)
                up_v(f, 1)
                queries(a, f)
                up_u(f, 2)
                up_v(f, 2)
                up_u(f, 3)
                logits(a, 0, f)
                up_v(f, 3)
                turn_rw(a, f)
                down(f, 0, start=True)
                bias_and_residual(f)
                logits(a, 1, f)
                spread(f, 2)
                up_u(f, 4)
                spread(f, 3)
                up_v(f, 4)
                down(f, 1)
                turn_probs(a, 0, 0, f)
                logits(a, 2, f)
                turn_probs(a, 0, 1, f)
                down(f, 2)
                turn_probs(a, 0, 2, f)
                logits(a, 3, f)
                weigh(a, 0, f)
                for t in range(1, NT - 1):
                    n = 4 + t
                    up_u(f, n)
                    spread(f, n - 1)
                    turn_probs(a, t, 0, f)
                    logits(a, 2 * t + 2, f)
                    turn_probs(a, t, 1, f)
                    down(f, n - 2)
                    up_v(f, n)
                    turn_probs(a, t, 2, f)
                    logits(a, 2 * t + 3, f)
                    weigh(a, t, f)
                up_u(f, 7)
                spread(f, 6)
                turn_probs(a, NT - 1, 0, f)
                up_v(f, 7)
                turn_probs(a, NT - 1, 1, f)
                down(f, 5)
                up_u(f, 8)
                turn_probs(a, NT - 1, 2, f)
                weigh(a, NT - 1, f)
                for n in range(8, NFC):
                    if n > 8:
                        up_u(f, n)
                    spread(f, n - 1)
                    if n > 8:
                        down(f, n - 3)
                    if n == 12:
                        turn_x2(a)
                    up_v(f, n)
                    if n == 8:
                        turn_ao(a)
                    if n == 9:
                        project(a)
                down(f, 10)
                spread(f, 12)
                start_up(a)
                down(f, 11)
                down(f, 12, stop=True)

            def last(f):
                for n in range(1, NFC):
                    up_u(f, n)
                    if n >= 4:
                        spread(f, n - 1)
                    if n >= 5:
                        down(f, n - 3)
                    if n == 3:
                        turn_rw(None, f)
                    up_v(f, n)
                    if n == 2:
                        down(f, 0, start=True)
                    if n == 3:
                        spread(f, 2)
                        bias_and_residual(f)
                        down(f, 1)
                spread(f, 12)
                down(f, 10)
                down(f, 11)
                down(f, 12, stop=True)

            pipeline(pe, first, both, last)


def kernel(**inputs):
    import numpy as np
    import concourse.bacc as bacc
    from concourse.bass_utils import run_bass_kernel_spmd

    a = {k: np.asarray(v) for k, v in inputs.items()}
    f = np.float32

    def rows(v, n):
        flat = np.concatenate([v.reshape(-1), np.zeros(n * P - v.size, f)])
        return flat.reshape(n, P).T

    x = a["x"].reshape(B, NT, P, D).transpose(0, 2, 1, 3).reshape(B, P, NT * D)
    ctx = a["ctx_1024"].transpose(2, 0, 1)
    ctx_t = ctx.reshape(D, B * Z)

    def up(w, sw):
        return np.concatenate([w.transpose(1, 0, 2).reshape(D, E * HID), sw], axis=1)

    w2 = np.concatenate([a["L0_ffn_w2"].reshape(E * HID, D), a["L0_ffn_sw2"], np.zeros((FP - (E + 1) * HID, D), f)])
    w2 = w2.reshape(NFC, P, D).transpose(1, 0, 2).reshape(P, FP)
    b1 = np.concatenate([a["L0_ffn_b1"].reshape(-1), a["L0_ffn_sb1"]])
    b3 = np.concatenate([a["L0_ffn_b3"].reshape(-1), a["L0_ffn_sb3"]])
    vecs = np.concatenate([
        a["L0_xattn_b_q"][:, None], a["L0_xattn_b_kv"][:D, None], a["L0_xattn_b_kv"][D:, None], rows(b1, NFC), rows(b3, NFC),
        np.broadcast_to(a["L0_xattn_b_out"], (P, D)), np.broadcast_to(a["L0_ffn_gate_b"], (P, E)),
    ], axis=1)
    zrow = np.arange(HZP).reshape(NZC, P).T // Z
    consts = np.concatenate([
        np.eye(P, dtype=f),
        (np.arange(P)[:, None] // HD == np.arange(HEADS)).astype(f),
        np.where(np.arange(Z)[None, :] >= np.arange(P)[:, None], f(MASK), f(0)),
        (zrow[:, :, None] == np.arange(HEADS)).astype(f).reshape(P, NZC * HEADS),
        np.broadcast_to(np.tril(np.ones((E, E), f), -1).reshape(-1), (P, E * E)),
    ], axis=1)
    sel_rows = np.where(np.arange(NEC * P)[None, :] // HID == np.arange(E)[:, None], f(0.5), f(0))

    arrays = {
        "x": x, "ctx_t": ctx_t, "w_q": a["L0_xattn_w_q"], "w_kv": a["L0_xattn_w_kv"],
        "w_out": a["L0_xattn_w_out"], "gate_wt": a["L0_ffn_gate_w"].T,
        "w1": up(a["L0_ffn_w1"], a["L0_ffn_sw1"]), "w3": up(a["L0_ffn_w3"], a["L0_ffn_sw3"]), "w2": w2,
        "b2": np.concatenate([a["L0_ffn_b2"], a["L0_ffn_sb2"][None]]), "vecs": vecs, "consts": consts, "sel_rows": sel_rows,
    }
    arrays = {k: np.ascontiguousarray(v) for k, v in arrays.items()}
    nc = bacc.Bacc("TRN2", target_bir_lowering=False, num_devices=1)
    args = [nc.dram_tensor(k, v.shape, mybir.dt.from_np(v.dtype), kind="ExternalInput").ap() for k, v in arrays.items()]
    out = nc.dram_tensor("out", (B, D, S), mybir.dt.float32, kind="ExternalOutput").ap()
    build(nc, *args, out)
    r = run_bass_kernel_spmd(nc, [arrays], core_ids=[0])
    return r.results[0]["out"].transpose(0, 2, 1)
```
